# Optimizing a Trainium2 kernel written in Bass

```python
import numpy as np
import jax
import jax.numpy as jnp

def _softmax(x, axis=-1):
    return jax.nn.softmax(x, axis=axis)

def _gelu(x):
    return jax.nn.gelu(x, approximate=True)

def _silu(x):
    return jax.nn.silu(x)

def _sigmoid(x):
    return jax.nn.sigmoid(x)

def _layernorm(x, axis=-1, eps=1e-05):
    m = jnp.mean(x, axis=axis, keepdims=True)
    v = jnp.var(x, axis=axis, keepdims=True)
    return (x - m) / jnp.sqrt(v + eps)

def _scatter_add(tgt, idx, src, axis=0):
    return tgt.at[idx].add(src)

def _segment_sum(src, seg, n):
    return jax.ops.segment_sum(src, seg, n)
kernel_name = 'mk_perceiver_d1_seqx_r4_25cbda'

def setup_inputs(seed: int=0):
    np.random.seed(seed)
    _w = jnp.asarray

    def _rec_inputs():
        import jax
        import jax.numpy as jnp
        _rk = jax.random.key(seed)
        x = -0.0002928 + 1 * jax.random.normal(jax.random.fold_in(_rk, 1), (4, 256, 256), jnp.float32)
        _lenS = 256 - jax.random.randint(jax.random.fold_in(_rk, 7), (4,), 0, max(1, 256 // 4) + 1, jnp.int32)
        _lenS2 = 4096 - jax.random.randint(jax.random.fold_in(_rk, 8), (4,), 0, max(1, 4096 // 4) + 1, jnp.int32)
        _ctx_1024P = jax.random.normal(jax.random.fold_in(_rk, 11), (4, 16, 256), jnp.float32)
        _ctx_1024c = jax.random.dirichlet(jax.random.fold_in(_rk, 511), 0.3 * jnp.ones((16,), jnp.float32), (4, 4096))
        _ctx_1024t = jnp.einsum('bsk,bkd->bsd', _ctx_1024c, _ctx_1024P)
        _ctx_1024t = _ctx_1024t * jax.lax.rsqrt(jnp.mean(jnp.square(_ctx_1024t)) + 1e-12) * 0.953939
        ctx_1024 = -1.39393e-06 + 0.999914 * (_ctx_1024t + 0.3 * jax.random.normal(jax.random.fold_in(_rk, 611), (4, 4096, 256), jnp.float32))
        _validS = jnp.arange(256)[None, :] < _lenS[:, None]
        _validS2 = jnp.arange(4096)[None, :] < _lenS2[:, None]
        _causal = jnp.tril(jnp.ones((256, 256), dtype=bool))
        mask_Bx1x1xS2_ik0 = jnp.where(jnp.broadcast_to(_validS2[:, None, None, :], (4, 1, 1, 4096)), 0, 1).astype(jnp.int32)
        return (x, ctx_1024, mask_Bx1x1xS2_ik0)
    x, ctx_1024, mask_Bx1x1xS2_ik0 = _rec_inputs()

    def _L0_xattn_setup():
        import jax, jax.numpy as jnp
        import numpy as np
        D_MODEL = 256
        NUM_HEADS = 16
        DEPTH = D_MODEL // NUM_HEADS
        B, S = (2, 512)
        NEG_BIG = -1000000000.0

        def _split_heads(x, b):
            return x.reshape(b, -1, NUM_HEADS, DEPTH).transpose(0, 2, 1, 3)
        key = jax.random.key(seed)
        ks = jax.random.split(key, 12)
        scale = 1.0 / np.sqrt(D_MODEL)
        inp = {'query': jax.random.normal(ks[0], (B, S, D_MODEL), jnp.float32), 'key': jax.random.normal(ks[1], (B, S, D_MODEL), jnp.float32), 'value': jax.random.normal(ks[2], (B, S, D_MODEL), jnp.float32), 'mask': jax.random.randint(ks[3], (B, 1, 1, S), 0, 2, jnp.int32), 'Wq': jax.random.normal(ks[4], (D_MODEL, D_MODEL), jnp.float32) * scale, 'bq': jnp.zeros((D_MODEL,), jnp.float32), 'Wk': jax.random.normal(ks[5], (D_MODEL, D_MODEL), jnp.float32) * scale, 'bk': jnp.zeros((D_MODEL,), jnp.float32), 'Wv': jax.random.normal(ks[6], (D_MODEL, D_MODEL), jnp.float32) * scale, 'bv': jnp.zeros((D_MODEL,), jnp.float32), 'Wo': jax.random.normal(ks[7], (D_MODEL, D_MODEL), jnp.float32) * scale, 'bo': jnp.zeros((D_MODEL,), jnp.float32)}
        return inp
    _L0_xattn_all = _L0_xattn_setup()
    _L0_xattn_in = {k: v for k, v in _L0_xattn_all.items() if k in ('Wq', 'bq', 'Wk', 'bk', 'Wv', 'bv', 'Wo', 'bo')}
    del _L0_xattn_all

    def _L0_attn_setup():
        import jax, jax.numpy as jnp
        import numpy as np
        import math
        N_EMBD = 256
        N_HEAD = 16
        HEAD = N_EMBD // N_HEAD
        LAMBDA_INIT = 0.8 - 0.6 * math.exp(-0.3 * (4 - 1))
        EPS = 1e-05
        key = jax.random.key(seed)
        ks = jax.random.split(key, 12)
        s = 1.0 / math.sqrt(N_EMBD)
        inp = {'x': jax.random.normal(ks[0], (2, 512, N_EMBD), dtype=jnp.float32), 'q1_w': jax.random.normal(ks[1], (N_EMBD, N_EMBD), dtype=jnp.float32) * s, 'q2_w': jax.random.normal(ks[2], (N_EMBD, N_EMBD), dtype=jnp.float32) * s, 'k1_w': jax.random.normal(ks[3], (N_EMBD, N_EMBD), dtype=jnp.float32) * s, 'k2_w': jax.random.normal(ks[4], (N_EMBD, N_EMBD), dtype=jnp.float32) * s, 'v_w': jax.random.normal(ks[5], (N_EMBD, 2 * N_EMBD), dtype=jnp.float32) * s, 'c_w': jax.random.normal(ks[6], (2 * N_EMBD, N_EMBD), dtype=jnp.float32) * (1.0 / math.sqrt(2 * N_EMBD)), 'lambda_q1': jax.random.normal(ks[7], (N_HEAD, HEAD), dtype=jnp.float32) * 0.1, 'lambda_k1': jax.random.normal(ks[8], (N_HEAD, HEAD), dtype=jnp.float32) * 0.1, 'lambda_q2': jax.random.normal(ks[9], (N_HEAD, HEAD), dtype=jnp.float32) * 0.1, 'lambda_k2': jax.random.normal(ks[10], (N_HEAD, HEAD), dtype=jnp.float32) * 0.1}
        return inp
    _L0_attn_all = _L0_attn_setup()
    _L0_attn_in = {k: v for k, v in _L0_attn_all.items() if k in ('q1_w', 'q2_w', 'k1_w', 'k2_w', 'v_w', 'c_w', 'lambda_q1', 'lambda_k1', 'lambda_q2', 'lambda_k2')}
    del _L0_attn_all

    def _L0_ffn_setup():
        import jax, jax.numpy as jnp
        import numpy as np
        S, B, D, E, C, FF = (512, 4, 256, 8, 512, 1024)
        N = S * B
        key = jax.random.key(seed)
        ks = jax.random.split(key, 7)
        return {'hidden_states': jax.random.normal(ks[0], (S, B, D), dtype=jnp.float32), 'combine_weights': jax.random.uniform(ks[1], (N, E), dtype=jnp.float32), 'top_idx': jax.random.randint(ks[2], (C, E), 0, N, dtype=jnp.int64), 'W1': jax.random.normal(ks[3], (E, D, FF), dtype=jnp.float32) * (1.0 / np.sqrt(D)), 'b1': jnp.zeros((E, FF), dtype=jnp.float32), 'W2': jax.random.normal(ks[4], (E, FF, D), dtype=jnp.float32) * (1.0 / np.sqrt(FF)), 'b2': jnp.zeros((E, D), dtype=jnp.float32)}
    _L0_ffn_all = _L0_ffn_setup()
    _L0_ffn_in = {k: v for k, v in _L0_ffn_all.items() if k in ('combine_weights', 'top_idx', 'W1', 'b1', 'W2', 'b2')}
    del _L0_ffn_all
    return {'x': x, 'ctx_1024': ctx_1024, 'mask_Bx1x1xS2_ik0': mask_Bx1x1xS2_ik0, 'L0_xattn_Wq': _L0_xattn_in['Wq'], 'L0_xattn_bq': _L0_xattn_in['bq'], 'L0_xattn_Wk': _L0_xattn_in['Wk'], 'L0_xattn_bk': _L0_xattn_in['bk'], 'L0_xattn_Wv': _L0_xattn_in['Wv'], 'L0_xattn_bv': _L0_xattn_in['bv'], 'L0_xattn_Wo': _L0_xattn_in['Wo'], 'L0_xattn_bo': _L0_xattn_in['bo'], 'L0_attn_q1_w': _L0_attn_in['q1_w'], 'L0_attn_q2_w': _L0_attn_in['q2_w'], 'L0_attn_k1_w': _L0_attn_in['k1_w'], 'L0_attn_k2_w': _L0_attn_in['k2_w'], 'L0_attn_v_w': _L0_attn_in['v_w'], 'L0_attn_c_w': _L0_attn_in['c_w'], 'L0_attn_lambda_q1': _L0_attn_in['lambda_q1'], 'L0_attn_lambda_k1': _L0_attn_in['lambda_k1'], 'L0_attn_lambda_q2': _L0_attn_in['lambda_q2'], 'L0_attn_lambda_k2': _L0_attn_in['lambda_k2'], 'L0_ffn_combine_weights': _L0_ffn_in['combine_weights'], 'L0_ffn_top_idx': _L0_ffn_in['top_idx'], 'L0_ffn_W1': _L0_ffn_in['W1'], 'L0_ffn_b1': _L0_ffn_in['b1'], 'L0_ffn_W2': _L0_ffn_in['W2'], 'L0_ffn_b2': _L0_ffn_in['b2']}

def reference(x, ctx_1024, mask_Bx1x1xS2_ik0, L0_xattn_Wq, L0_xattn_bq, L0_xattn_Wk, L0_xattn_bk, L0_xattn_Wv, L0_xattn_bv, L0_xattn_Wo, L0_xattn_bo, L0_attn_q1_w, L0_attn_q2_w, L0_attn_k1_w, L0_attn_k2_w, L0_attn_v_w, L0_attn_c_w, L0_attn_lambda_q1, L0_attn_lambda_k1, L0_attn_lambda_q2, L0_attn_lambda_k2, L0_ffn_combine_weights, L0_ffn_top_idx, L0_ffn_W1, L0_ffn_b1, L0_ffn_W2, L0_ffn_b2):
    import jax
    import jax.numpy as jnp

    def _L0_xattn_ref(query, key, value, mask, Wq, bq, Wk, bk, Wv, bv, Wo, bo):
        import jax, jax.numpy as jnp
        import numpy as np
        D_MODEL = 256
        NUM_HEADS = 16
        DEPTH = D_MODEL // NUM_HEADS
        B, S = (2, 512)
        NEG_BIG = -1000000000.0

        def _split_heads(x, b):
            return x.reshape(b, -1, NUM_HEADS, DEPTH).transpose(0, 2, 1, 3)
        b = query.shape[0]
        q = _split_heads(query @ Wq + bq, b)
        k = _split_heads(key @ Wk + bk, b)
        v = _split_heads(value @ Wv + bv, b)
        logits = jnp.einsum('bhqd,bhkd->bhqk', q, k) / jnp.sqrt(jnp.asarray(DEPTH, q.dtype))
        logits = logits.astype(jnp.float32) + mask.astype(jnp.float32) * NEG_BIG
        attn = jax.nn.softmax(logits, axis=-1)
        ctx = jnp.einsum('bhqk,bhkd->bhqd', attn, v.astype(jnp.float32))
        ctx = ctx.astype(q.dtype)
        concat = ctx.transpose(0, 2, 1, 3).reshape(b, -1, D_MODEL)
        return concat @ Wo + bo

    def _L0_attn_ref(x, q1_w, q2_w, k1_w, k2_w, v_w, c_w, lambda_q1, lambda_k1, lambda_q2, lambda_k2):
        import jax, jax.numpy as jnp
        import numpy as np
        import math
        N_EMBD = 256
        N_HEAD = 16
        HEAD = N_EMBD // N_HEAD
        LAMBDA_INIT = 0.8 - 0.6 * math.exp(-0.3 * (4 - 1))
        EPS = 1e-05
        B, T, C = x.shape
        H, hs = (N_HEAD, HEAD)

        def heads(w, d):
            return (x @ w).reshape(B, T, H, d).transpose(0, 2, 1, 3)
        q1 = heads(q1_w, hs)
        q2 = heads(q2_w, hs)
        k1 = heads(k1_w, hs)
        k2 = heads(k2_w, hs)
        v = heads(v_w, 2 * hs)
        scale = 1.0 / math.sqrt(hs)
        causal = jnp.tril(jnp.ones((T, T), dtype=bool))
        neg = jnp.float32(-jnp.inf)
        att1 = jnp.einsum('bhqd,bhkd->bhqk', q1, k1) * scale
        att2 = jnp.einsum('bhqd,bhkd->bhqk', q2, k2) * scale
        att1 = jax.nn.softmax(jnp.where(causal, att1, neg), axis=-1)
        att2 = jax.nn.softmax(jnp.where(causal, att2, neg), axis=-1)
        lam1 = jnp.exp(jnp.sum(lambda_q1 * lambda_k1, axis=-1))
        lam2 = jnp.exp(jnp.sum(lambda_q2 * lambda_k2, axis=-1))
        lam = (lam1 - lam2 + LAMBDA_INIT)[None, :, None, None]
        att = att1 - lam * att2
        y = jnp.einsum('bhqk,bhkd->bhqd', att, v)
        mu = jnp.mean(y, axis=-1, keepdims=True)
        var = jnp.mean(jnp.square(y - mu), axis=-1, keepdims=True)
        y = (y - mu) / jnp.sqrt(var + EPS)
        y = y * (1.0 - LAMBDA_INIT)
        y = y.transpose(0, 2, 1, 3).reshape(B, T, 2 * C)
        return y @ c_w

    def _L0_ffn_ref(hidden_states, combine_weights, top_idx, W1, b1, W2, b2):
        import jax, jax.numpy as jnp
        import numpy as np
        S, B, D, E, C, FF = (512, 4, 256, 8, 512, 1024)
        N = S * B
        s, b, d = hidden_states.shape
        x = hidden_states.reshape(-1, d)
        tok = top_idx.T
        gathered = x[tok]
        h = jax.nn.gelu(jnp.einsum('ecd,edf->ecf', gathered, W1) + b1[:, None, :])
        out_e = jnp.einsum('ecf,efd->ecd', h, W2) + b2[:, None, :]
        e_ids = jnp.arange(tok.shape[0])[:, None]
        w = combine_weights[tok, e_ids]
        weighted = (out_e * w[..., None]).reshape(-1, d)
        out = jnp.zeros_like(x).at[tok.reshape(-1)].add(weighted)
        return out.reshape(s, b, d)
    x = x + _L0_xattn_ref(_layernorm(x, axis=-1), ctx_1024, ctx_1024, mask_Bx1x1xS2_ik0, L0_xattn_Wq, L0_xattn_bq, L0_xattn_Wk, L0_xattn_bk, L0_xattn_Wv, L0_xattn_bv, L0_xattn_Wo, L0_xattn_bo)
    x = x + _L0_attn_ref(_layernorm(x, axis=-1), L0_attn_q1_w, L0_attn_q2_w, L0_attn_k1_w, L0_attn_k2_w, L0_attn_v_w, L0_attn_c_w, L0_attn_lambda_q1, L0_attn_lambda_k1, L0_attn_lambda_q2, L0_attn_lambda_k2)
    x = x + _L0_ffn_ref(_layernorm(x, axis=-1), L0_ffn_combine_weights, L0_ffn_top_idx, L0_ffn_W1, L0_ffn_b1, L0_ffn_W2, L0_ffn_b2)
    return x

_drawn_inputs = setup_inputs


def setup_inputs(seed=0):
    import zlib

    import numpy as np

    out = dict(_drawn_inputs(seed))
    spreads = {'L0_xattn_bq': (0.0, 0.33),
     'L0_xattn_bk': (0.0, 0.8),
     'L0_xattn_bv': (0.0, 0.1),
     'L0_xattn_bo': (0.0, 0.1),
     'L0_ffn_b1': (0.0, 0.1),
     'L0_ffn_b2': (0.0, 0.1)}
    factors = {'L0_attn_lambda_q1': 2.92,
     'L0_attn_lambda_k1': 2.895,
     'L0_attn_lambda_q2': 3.096,
     'L0_attn_lambda_k2': 3.044}
    for name, (base, spread) in spreads.items():
        noise = np.random.default_rng([zlib.crc32(name.encode()), seed]).standard_normal(out[name].shape)
        drawn = base * np.exp(spread * noise) if base else spread * noise
        out[name] = jnp.asarray(drawn.astype(out[name].dtype))
    for name, factor in factors.items():
        out[name] = (out[name] * factor).astype(out[name].dtype)
    return out
```

```python
import math
from contextlib import ExitStack

import concourse.bass as bass
from concourse import mybir

F32 = mybir.dt.float32
F32R = mybir.dt.float32r
BF16 = mybir.dt.bfloat16
I32 = mybir.dt.int32
ALU = mybir.AluOpType
ACT = mybir.ActivationFunctionType
AX = mybir.AxisListType

P = 128
D = 256
DC = D // P
H = 16
DH = D // H
LN_EPS = 1e-5

B = 4
NQ = 256
NK = 4096
NTOK = B * NQ


ROWS = 52


def query_stage(nc, x, Wq, bq, mask, q_stacks, mask_rows):
    NT = NTOK // P
    NPAIR = H // 2
    with ExitStack() as ctx:
        def sb(name, shape, dt):
            return ctx.enter_context(nc.sbuf_tensor(name, shape, dt))

        def sem(name):
            return ctx.enter_context(nc.semaphore(name))

        x_in = sb("x_in", [P, NT, D], F32)
        xn = sb("xn", [P, NT, D], F32)
        xnT = sb("xnT", [P, DC, NTOK], F32)
        stats = sb("stats", [P, NT, 6], F32)
        mv = sb("mv", [P, NT, 2], F32)
        rstd = sb("rstd", [P, NT], F32)
        var_eps = sb("var_eps", [P, NT], F32)
        std = sb("std", [P, NT], F32)
        wq = sb("wq", [P, DC, D], F32)
        wq_rep = sb("wq_rep", [P, DC, H, 64], F32)
        bq_rep = sb("bq_rep", [P, NPAIR], F32)
        bq_scaled = sb("bq_scaled", [P, NPAIR], F32)
        lo_rows = sb("lo_rows", [P, 1], F32)
        consts = sb("consts", [P, NPAIR], F32)
        minus1 = sb("minus1", [P, 1], F32)
        ident = sb("ident_q", [P, P], F32)
        mask_i = sb("mask_i", [P, P], I32)
        mask_f = sb("mask_f", [P, P], F32)
        mask_hi = sb("mask_hi", [P, P], F32R)
        mask_lo = sb("mask_lo", [P, P], F32R)
        q_full = [sb(f"q_full{i}", [P, 512], F32) for i in range(2)]
        q_hi = [sb(f"q_hi{i}", [P, 512], F32R) for i in range(2)]
        q_out = [sb(f"q_out{i}", [P, 512], F32R) for i in range(2)]
        pt = [ctx.enter_context(nc.psum_tensor(f"pt{i}", [P, 512], F32)) for i in range(2)]
        pq = [ctx.enter_context(nc.psum_tensor(f"pq{i}", [P, 512], F32)) for i in range(2)]

        x_loaded = sem("x_loaded")
        w_loaded = sem("w_loaded")
        b_loaded = sem("b_loaded")
        mask_loaded = sem("mask_loaded")
        consts_set = sem("consts_set")
        ident_set = sem("ident_set")
        stats_done = sem("stats_done")
        std_done = sem("std_done")
        norm_done = sem("norm_done")
        rep_done = sem("rep_done")
        bias_done = sem("bias_done")
        mask_done = sem("mask_done")
        turned = sem("turned")
        turned_read = sem("turned_read")
        q_ready = sem("q_ready")
        full_done = sem("full_done")
        hi_done = sem("hi_done")
        out_done = sem("out_done")
        stored = [sem(f"stored{i}") for i in range(2)]
        mask_stored = sem("mask_stored")
        block = ctx.enter_context(nc.Block())

        @block.sync
        def _(sp):
            sp.dma_start(x_in[:], x.rearrange("b (t p) d -> p (b t) d", p=P)).then_inc(x_loaded, 16)
            sp.dma_start(wq[:], Wq.rearrange("(c p) n -> p c n", p=P)).then_inc(w_loaded, 16)
            sp.dma_start(mask_i[:], mask.rearrange("b u v (t f) -> (b u v t) f", f=P)).then_inc(mask_loaded, 16)
            sp.wait_ge(consts_set, 4)
            for j in range(2):
                for r in range(3):
                    row = 64 * j + 16 * r
                    sp.dma_start(bq_rep[row:row + DH, :], bq.rearrange("(n j d) -> j d n", j=2, d=DH)[j],
                                 allow_slow_non_contiguous=True).then_inc(b_loaded, 16)
                sp.dma_start(bq_rep[64 * j + 50:64 * j + 52, :], consts[0:2, :]).then_inc(b_loaded, 16)
                sp.dma_start(lo_rows[64 * j + 32:64 * j + 48, :], minus1[0:16, :]).then_inc(b_loaded, 16)
            sp.wait_ge(mask_done, 3)
            sp.dma_start(mask_rows[0].rearrange("b (t f) -> (b t) f", f=P), mask_hi[:].bitcast(F32)).then_inc(mask_stored, 16)
            sp.dma_start(mask_rows[1].rearrange("b (t f) -> (b t) f", f=P), mask_lo[:].bitcast(F32)).then_inc(mask_stored, 16)
            for n in range(2 * NPAIR):
                pair, half = n // 2, n % 2
                sp.wait_ge(out_done, n + 1)
                sp.dma_start(q_stacks[2 * half:2 * half + 2, pair // 2, :, pair % 2, :].rearrange("b p q -> p b q"),
                             q_out[n % 2][:].bitcast(F32).rearrange("p (b q) -> p b q", b=2)).then_inc(stored[n % 2], 16)
            sp.wait_ge(mask_stored, 32)
            for i in range(2):
                sp.wait_ge(stored[i], 16 * NPAIR)

        @block.gpsimd
        def _(pool):
            pool.memset(consts[:], 4.0).then_inc(consts_set, 1)
            pool.memset(minus1[:], -1.0).then_inc(consts_set, 1)
            pool.memset(bq_rep[:], 0.0).then_inc(consts_set, 1)
            pool.memset(lo_rows[:], 0.0).then_inc(consts_set, 1)
            pool.memset(ident[:], 0.0).then_inc(ident_set, 1)
            pool.wait_ge(ident_set, 1)
            pool.affine_select(out=ident[:], in_=ident[:], compare_op=ALU.not_equal, fill=1.0, base=0,
                               pattern=[[-1, P]], channel_multiplier=1).then_inc(ident_set, 1)
            pool.memset(wq_rep[:], 0.0).then_inc(rep_done, 1)
            pool.wait_ge(w_loaded, 16)
            pool.wait_ge(rep_done, 1)
            for c in range(DC):
                for r in range(3):
                    pool.tensor_copy(wq_rep[:, c, :, 16 * r:16 * r + DH],
                                     wq[:, c, :].rearrange("p (h d) -> p h d", d=DH)).then_inc(rep_done, 1)

        @block.vector
        def _(dve):
            dve.wait_ge(mask_loaded, 16)
            dve.tensor_scalar(mask_f[:], mask_i[:], -1e9, None, ALU.mult).then_inc(mask_done, 1)
            dve.wait_ge(mask_done, 1)
            dve.tensor_copy(mask_hi[:], mask_f[:]).then_inc(mask_done, 1)
            dve.wait_ge(mask_done, 2)
            dve.tensor_sub(mask_lo[:], mask_f[:], mask_hi[:].bitcast(F32)).then_inc(mask_done, 1)
            dve.wait_ge(x_loaded, 16)
            for t in range(NT):
                dve.bn_stats(stats[:, t, :], x_in[:, t, :]).then_inc(stats_done, 1)
            for t in range(NT):
                dve.wait_ge(stats_done, t + 1)
                dve.bn_aggr(mv[:, t, :], stats[:, t, :]).then_inc(stats_done, 1)
            dve.wait_ge(stats_done, 2 * NT)
            dve.tensor_scalar(var_eps[:], mv[:, :, 1], LN_EPS, None, ALU.add).then_inc(stats_done, 1)
            dve.wait_ge(std_done, 1)
            dve.reciprocal(rstd[:], std[:]).then_inc(stats_done, 1)
            dve.wait_ge(stats_done, 2 * NT + 2)
            for t in range(NT):
                dve.tensor_scalar(xn[:, t, :], x_in[:, t, :], mv[:, t, 0:1], rstd[:, t:t + 1],
                                  ALU.subtract, ALU.mult).then_inc(norm_done, 1)
            dve.wait_ge(b_loaded, 160)
            dve.tensor_scalar(bq_scaled[:], bq_rep[:], DH ** -0.5, None, ALU.mult).then_inc(bias_done, 1)
            for n in range(NT // 2 * DC):
                c, t4 = n % DC, n // DC
                if t4 * 4 >= NT:
                    break
                dve.wait_ge(turned, n + 1)
                dve.tensor_copy(xnT[:, c, t4 * 512:t4 * 512 + 512], pt[n % 2][:]).then_inc(turned_read, 1)
            for n in range(2 * NPAIR):
                dve.wait_ge(hi_done, n + 1)
                if n >= 2:
                    dve.wait_ge(stored[n % 2], 16 * (n // 2))
                dve.scalar_tensor_tensor(q_out[n % 2][:], q_hi[n % 2][:].bitcast(F32), lo_rows[:, 0:1],
                                         q_full[n % 2][:], ALU.mult, ALU.add).then_inc(out_done, 1)

        @block.tensor
        def _(pe):
            pe.wait_ge(ident_set, 2)
            for n in range(NT // 4 * DC):
                c, t4 = n % DC, n // DC
                pe.wait_ge(norm_done, 4 * t4 + 4)
                if n >= 2:
                    pe.wait_ge(turned_read, n - 1)
                for t in range(4):
                    mm = pe.transpose(pt[n % 2][:, t * P:(t + 1) * P], xn[:, 4 * t4 + t, c * P:(c + 1) * P], ident[:])
                mm.then_inc(turned, 1)
            pe.wait_ge(turned_read, NT // 4 * DC)
            pe.wait_ge(rep_done, 7)
            for n in range(2 * NPAIR):
                pair, half = n // 2, n % 2
                if n >= 2:
                    pe.wait_ge(full_done, n - 1)
                for c in range(DC):
                    mm = pe.matmul(pq[n % 2][:], wq_rep[:, c, 2 * pair:2 * pair + 2, :].rearrange("p h r -> p (h r)"),
                                   xnT[:, c, half * 512:half * 512 + 512], start=(c == 0), stop=(c == DC - 1))
                mm.then_inc(q_ready, 1)

        @block.scalar
        def _(act):
            act.wait_ge(stats_done, 2 * NT + 1)
            act.activation(std[:], var_eps[:], ACT.Sqrt).then_inc(std_done, 1)
            act.wait_ge(bias_done, 1)
            for n in range(2 * NPAIR):
                pair = n // 2
                act.wait_ge(q_ready, n + 1)
                if n >= 2:
                    act.wait_ge(out_done, n - 1)
                act.activation(q_full[n % 2][:], pq[n % 2][:], ACT.Identity, bias=bq_scaled[:, pair:pair + 1],
                               scale=DH ** -0.5).then_inc(full_done, 1)
                act.wait_ge(full_done, n + 1)
                act.activation(q_hi[n % 2][:], q_full[n % 2][:], ACT.Copy).then_inc(hi_done, 1)


QU = 4
KT = NK // P
STEPS = QU * KT
TAIL = STEPS
NMAX = 64
MAX_STEPS = 28


def misc_plan(last):
    jobs = []
    for q in range(QU):
        s0 = q * KT
        if q > 0:
            jobs.append((s0 + 3, "X", q - 1, 0))
        if q == 0:
            jobs += [(s0 + 5 + 2 * i, "K", 2, i) for i in range(8)]
        elif last:
            pass
        elif q == 1:
            jobs += [(s0 + (t if t < 3 else t + 1), "T", QU, t) for t in range(16)]
        elif q == 2:
            jobs += [(s0 + 5 + 2 * i, "K", QU, i) for i in range(8)]
        else:
            jobs += [(s0 + 4 + 2 * j, "V", QU, j) for j in range(16)]
        if not (last and q == 3):
            jobs.append((s0 + MAX_STEPS + 1, "M", q + 1, 0))
    jobs += [(TAIL, "X", 3, 0), (TAIL, "W", 0, 0)]
    jobs = [(min(s, TAIL), *rest) for s, *rest in jobs]
    order = sorted(range(len(jobs)), key=lambda n: (jobs[n][0], jobs[n][1] != "X", n))
    return [jobs[n] for n in order]


FIRST_JOBS = [j for i in range(8) for j in (("T", 0, 2 * i), ("T", 0, 2 * i + 1), ("K", 0, i))]
FIRST_JOBS += [("V", 0, j) for j in range(16)] + [("M", 0, 0)]

JOB_COST = {"T": 0.6, "K": 1.8, "V": 1.8, "M": 0.2, "X": 0.5, "W": 0.0}


def max_jobs_at(q, kt):
    cost = [1.4] * MAX_STEPS
    for step, kind, _, _ in misc_plan(False):
        if step // KT == q and step % KT < MAX_STEPS:
            cost[step % KT] += JOB_COST[kind]
    bounds = [round(NMAX * sum(cost[:n]) / sum(cost)) for n in range(MAX_STEPS + 1)]
    return range(bounds[kt], bounds[kt + 1]) if kt < MAX_STEPS else range(0)


def max_job(n):
    return n // 8, (n // 4) % 2, (n // 2) % 2, n % 2


def cross_stage(nc, x, ctx_in, Wk, bk, Wv, bv, Wo, bo, q_stacks, mask_rows, x1):
    NJ = len(misc_plan(False))
    NF = len(FIRST_JOBS)
    with ExitStack() as ctx:
        def sb(name, shape, dt):
            return ctx.enter_context(nc.sbuf_tensor(name, shape, dt))

        def sem(name):
            return ctx.enter_context(nc.semaphore(name))

        def psum(name, shape):
            return ctx.enter_context(nc.psum_tensor(name, shape, F32))

        stack = [sb(f"stack{i}", [P, 2, NK], F32R) for i in range(2)]
        k_hi = sb("k_hi", [P, NK], F32R)
        k_lo = sb("k_lo", [P, NK], F32R)
        ctxT = sb("ctxT", [P, DC, NK], F32)
        raw = [sb(f"raw{i}", [P, 2, D], F32) for i in range(2)]
        val = sb("val", [P, KT, H, DH + 1], F32)
        qs = sb("qs", [P, QU, 2, NQ], F32R)
        prob = [sb(f"prob{i}", [P, 2, 2, NQ], F32) for i in range(2)]
        wk = sb("wk", [P, DC, D], F32)
        wv = sb("wv", [P, DC, D], F32)
        wo = sb("wo", [P, QU, D], F32)
        bk_u = sb("bk_u", [P, 2], F32)
        bv_u = sb("bv_u", [P, QU], F32)
        bo_r = sb("bo_r", [1, D], F32)
        ones_r = sb("ones_r", [1, P], F32)
        ident = sb("ident", [P, P], F32)
        den_sel = sb("den_sel", [P, P], F32)
        max_parts = sb("max_parts", [P, 8, 8], F32)
        neg_max = sb("neg_max", [P, 8], F32)
        neg_hi = sb("neg_hi", [P, 8], F32R)
        neg_cols = sb("neg_cols", [P, 4, 2, 2], F32)
        neg_rows = sb("neg_rows", [16, P], F32R)
        head_out = sb("head_out", [P, NQ], F32)
        rden = sb("rden", [P, NQ], F32)
        normed = sb("normed", [P, NQ], F32)
        heads = sb("heads", [P, QU, NQ], F32)
        x_res = sb("x_res", [P, 2, D], F32)
        x_out = sb("x_out", [P, 2, D], F32)
        score = [psum(f"score{i}", [P, 2, 2, NQ]) for i in range(2)]
        mx = [psum(f"mx{i}", [P, 512]) for i in range(2)]
        misc = psum("misc", [P, 512])
        acc = psum("acc", [P, 512])

        w_loaded = sem("w_loaded_x")
        zeroed = sem("zeroed")
        consts_set = sem("consts_set_x")
        raw_loaded = [sem(f"raw_loaded{i}") for i in range(2)]
        q_loaded = [sem(f"q_loaded{i}") for i in range(QU)]
        k_stacked = [[sem(f"k_stacked{i}{h}") for h in range(2)] for i in range(2)]
        mask_stacked = [[sem(f"mask_stacked{i}{h}") for h in range(2)] for i in range(2)]
        neg_stacked = sem("neg_stacked")
        res_loaded = sem("res_loaded")
        x1_stored = sem("x1_stored")
        scored = sem("scored")
        exp_done = sem("exp_done")
        pv_done = sem("pv_done")
        max_ready = sem("max_ready")
        max_read = sem("max_read")
        misc_ready = sem("misc_ready")
        misc_read = sem("misc_read")
        khi_done = sem("khi_done")
        passed = sem("passed")
        neg_found = sem("neg_found")
        neg_split = sem("neg_split")
        neg_turnable = sem("neg_turnable")
        acc_read = sem("acc_read")
        normed_done = sem("normed_done")
        heads_done = sem("heads_done")
        block = ctx.enter_context(nc.Block())

        def index_of(jobs_list, kind, unit, i):
            return [j[-3:] for j in jobs_list].index((kind, unit, i))

        def job_count(b, last, kind, unit, i):
            return NF + b * NJ + index_of(misc_plan(last), kind, unit, i) + 1

        def first_count(kind, unit, i):
            return index_of(FIRST_JOBS, kind, unit, i) + 1

        def wait_apart(eng, sem, count):
            eng.wait_ge(sem, count)
            eng.sem_inc(passed, 1)

        def all_batches(eng, body):
            with eng.Fori(0, B - 1) as b:
                body(b, False)
            body(B - 1, True)

        @block.gpsimd
        def _(pool):
            pool.memset(ident[:], 0.0).then_inc(zeroed, 1)
            pool.memset(den_sel[:], 0.0).then_inc(zeroed, 1)
            pool.memset(head_out[:], 0.0).then_inc(zeroed, 1)
            pool.memset(wo[:], 0.0).then_inc(zeroed, 1)
            pool.memset(bv_u[:], 0.0).then_inc(zeroed, 1)
            pool.memset(ones_r[:], 1.0).then_inc(zeroed, 1)
            pool.wait_ge(zeroed, 2)
            pool.affine_select(out=ident[:], in_=ident[:], compare_op=ALU.not_equal, fill=1.0, base=0,
                               pattern=[[-1, P]], channel_multiplier=1).then_inc(consts_set, 1)
            v = den_sel[:].rearrange("p (h r) -> p h r", h=4)
            pool.affine_select(out=v, in_=v, compare_op=ALU.not_equal, fill=1.0, base=-DH,
                               pattern=[[-32, 4], [0, 32]], channel_multiplier=1).then_inc(consts_set, 1)
            pool.memset(stack[1][:].bitcast(F32), 1.0).then_inc(consts_set, 1)

            def load_ctx(b, t, free):
                if free is not None:
                    pool.wait_ge(misc_ready, free)
                pool.dma_start(raw[t % 2][:], ctx_in[b, 2 * P * t:2 * P * (t + 1), :]
                               .rearrange("(i p) d -> p i d", p=P)).then_inc(raw_loaded[t % 2], 16)

            def load_q(b, q):
                pool.dma_start(qs[:, q, :, :].bitcast(F32), q_stacks[b, q]).then_inc(q_loaded[q], 16)

            def load_mask(b, i, h):
                for j in range(2):
                    for pair in range(2):
                        pool.dma_start(stack[i][64 * j + 50:64 * j + 52, pair, h * 2048:(h + 1) * 2048].bitcast(F32),
                                       mask_rows[:, b, h * 2048:(h + 1) * 2048]).then_inc(mask_stacked[i][h], 16)

            load_ctx(0, 0, None)
            load_ctx(0, 1, None)
            pool.wait_ge(consts_set, 5)
            for i in range(2):
                for h in range(2):
                    load_mask(0, i, h)
            for q in range(QU):
                load_q(0, q)
            for t in range(2, 16):
                load_ctx(0, t, first_count("T", 0, t - 2))
            pool.dma_start(x_res[:], x[0].rearrange("(i p) d -> p i d", p=P)).then_inc(res_loaded, 16)

            def body(b, last):
                if last:
                    return
                load_ctx(b + 1, 0, NF + b * NJ)
                load_ctx(b + 1, 1, NF + b * NJ)
                pool.wait_ge(scored, STEPS * b + KT)
                load_q(b + 1, 0)
                for t in range(2, 16):
                    load_ctx(b + 1, t, job_count(b, False, "T", QU, t - 2))
                pool.wait_ge(scored, STEPS * b + 2 * KT)
                load_q(b + 1, 1)
                for i in range(2):
                    wait_apart(pool, scored, STEPS * b + KT * (i + 2) + KT // 2)
                    load_mask(b + 1, i, 0)
                    wait_apart(pool, scored, STEPS * b + KT * (i + 3))
                    load_mask(b + 1, i, 1)
                    load_q(b + 1, i + 2)
                pool.wait_ge(misc_read, job_count(b, False, "W", 0, 0))
                pool.dma_start(x_res[:], x[b + 1].rearrange("(i p) d -> p i d", p=P)).then_inc(res_loaded, 16)

            all_batches(pool, body)

        @block.sync
        def _(sp):
            sp.sem_inc(x1_stored, 16)
            sp.dma_start(wk[:], Wk.rearrange("(c p) n -> p c n", p=P)).then_inc(w_loaded, 16)
            sp.dma_start(wv[:], Wv.rearrange("(c p) n -> p c n", p=P)).then_inc(w_loaded, 16)
            sp.dma_start(bo_r[:], bo.rearrange("(a n) -> a n", a=1)).then_inc(w_loaded, 16)
            sp.dma_start(bk_u[:], bk.rearrange("(g p) -> p g", g=2), allow_slow_non_contiguous=True)\
                .then_inc(w_loaded, 16)
            sp.wait_ge(zeroed, 5)
            for hq in range(4):
                sp.dma_start(wo[32 * hq:32 * hq + DH, :, :], Wo.rearrange("(q h d) n -> h d q n", q=QU, h=4)[hq])\
                    .then_inc(w_loaded, 16)
                sp.dma_start(bv_u[32 * hq:32 * hq + DH, :], bv.rearrange("(q h d) -> h d q", q=QU, h=4)[hq],
                             allow_slow_non_contiguous=True).then_inc(w_loaded, 16)

            def stack_keys(q, h):
                for hq in range(4):
                    pair, j = hq // 2, hq % 2
                    i = q % 2
                    src = slice(64 * i + 16 * hq, 64 * i + 16 * hq + DH)
                    for r, part in enumerate((k_hi, k_lo, k_hi)):
                        sp.dma_start(stack[i][64 * j + 16 * r:64 * j + 16 * r + DH, pair, h * 2048:(h + 1) * 2048]
                                     .bitcast(F32), part[src, h * 2048:(h + 1) * 2048].bitcast(F32)).then_inc(k_stacked[i][h], 16)

            def stack_max(q):
                for hq in range(4):
                    pair, j = hq // 2, hq % 2
                    for qh in range(2):
                        row = 4 * hq + 2 * qh
                        sp.dma_start(qs[64 * j + 48:64 * j + 50, q, pair, qh * P:(qh + 1) * P].bitcast(F32),
                                     neg_rows[row:row + 2, :].bitcast(F32)).then_inc(neg_stacked, 16)

            sp.wait_ge(consts_set, 5)
            for h in range(2):
                sp.wait_ge(misc_read, first_count("K", 0, 4 * h + 3))
                stack_keys(0, h)
            for h in range(2):
                stack_keys(1, h)
            sp.wait_ge(misc_read, first_count("M", 0, 0))
            stack_max(0)

            def body(b, last):
                for q in range(QU):
                    if not (last and q >= 2):
                        if q % 2 == 0:
                            wait_apart(sp, misc_read, job_count(b, last, "K", q + 2, 7))
                        sp.wait_ge(scored, STEPS * b + KT * q + KT // 2)
                        stack_keys(q, 0)
                    if not (last and q == 3):
                        sp.wait_ge(misc_read, job_count(b, last, "M", q + 1, 0))
                        stack_max((q + 1) % QU)
                    if not (last and q >= 2):
                        sp.wait_ge(scored, STEPS * b + KT * (q + 1))
                        stack_keys(q, 1)
                sp.wait_ge(misc_read, job_count(b, last, "W", 0, 0))
                sp.dma_start(x1[b].rearrange("(i p) d -> p i d", p=P), x_out[:]).then_inc(x1_stored, 16)

            all_batches(sp, body)
            sp.wait_ge(x1_stored, 16 * (B + 1))

        @block.tensor
        def _(pe):
            pe.wait_ge(consts_set, 5)
            pe.wait_ge(w_loaded, 16 * 12)

            def job(count, kind, b, u, i, t_count):
                if not (isinstance(count, int) and count == 0):
                    pe.wait_ge(misc_read, count)
                if kind == "T":
                    pe.wait_ge(raw_loaded[i % 2], 16 * (8 * b + i // 2 + 1))
                    for t in range(2):
                        for c in range(DC):
                            mm = pe.transpose(misc[:, c * 256 + t * P:c * 256 + (t + 1) * P],
                                              raw[i % 2][:, t, c * P:(c + 1) * P], ident[:])
                elif kind == "K":
                    g = u % QU // 2
                    for c in range(DC):
                        mm = pe.matmul(misc[:], wk[:, c, P * g:P * (g + 1)], ctxT[:, c, i * 512:(i + 1) * 512],
                                       start=(c == 0), stop=(c == DC - 1))
                elif kind == "V":
                    for t in range(2):
                        for c in range(DC):
                            mm = pe.matmul(misc[:, t * 256:(t + 1) * 256], ctxT[:, c, (2 * i + t) * P:(2 * i + t + 1) * P],
                                           wv[:, c, :], start=(c == 0), stop=(c == DC - 1))
                elif kind == "M":
                    pe.wait_ge(neg_turnable, t_count)
                    mm = pe.transpose(misc[0:16, 0:P], neg_cols[:].rearrange("p a b c -> p (a b c)"), ident[:])
                elif kind == "X":
                    pe.wait_ge(acc_read, t_count)
                    mm = pe.matmul(misc[:, 0:NQ], den_sel[:], head_out[:], start=True, stop=True)
                elif kind == "W":
                    pe.wait_ge(heads_done, t_count)
                    for t in range(2):
                        out = misc[:, t * 256:(t + 1) * 256]
                        pe.matmul(out, ones_r[:], bo_r[:], start=True, stop=False)
                        for q in range(QU):
                            mm = pe.matmul(out, heads[:, q, t * P:(t + 1) * P], wo[:, q, :],
                                           start=False, stop=(q == QU - 1))
                mm.then_inc(misc_ready, 1)

            def max_tile(n, i, q, use, batch, count):
                chunk, pair, qh, j = max_job(n)
                if n % 32 == 0:
                    h = n // 32
                    pe.wait_ge(k_stacked[i][h], 16 * 12 * (use + 1))
                    if q < 2:
                        pe.wait_ge(mask_stacked[i][h], 64 * (batch + 1))
                if count is not None:
                    pe.wait_ge(max_read, count)
                pe.matmul(mx[j][:], qs[64 * j:64 * j + ROWS, q, pair, qh * P:(qh + 1) * P],
                          stack[i][64 * j:64 * j + ROWS, pair, chunk * 512:(chunk + 1) * 512],
                          start=True, stop=True).then_inc(max_ready, 1)

            def pv(b, s):
                q, kt = s // KT, s % KT
                pe.wait_ge(exp_done, STEPS * b + s + 1)
                if kt == 0 and q > 0:
                    pe.wait_ge(acc_read, 4 * b + q)
                for hq in range(4):
                    mm = pe.matmul(acc[32 * hq:32 * hq + DH + 1, 0:NQ], val[:, kt, 4 * q + hq, :],
                                   prob[s % 2][:, hq % 2, hq // 2, :], start=(kt == 0), stop=(kt == KT - 1))
                mm.then_inc(pv_done, 1)

            for n, (kind, u, i) in enumerate(FIRST_JOBS):
                if kind == "V":
                    if i == 0:
                        pe.wait_ge(q_loaded[0], 16)
                    for m in range(4 * i, 4 * i + 4):
                        max_tile(m, 0, 0, 0, 0, m - 1 if m >= 2 else None)
                job(n, kind, 0, u, i, 2)

            def body(b, last):
                plan = misc_plan(last)
                count = 0
                pe.wait_ge(misc_read, NF + b * NJ)
                for s in range(STEPS + 1):
                    q, kt = s // KT, s % KT
                    if s < STEPS:
                        if kt == 0:
                            pe.wait_ge(neg_stacked, 16 * 8 * (4 * b + q + 1))
                        if s >= 2:
                            pe.wait_ge(exp_done, STEPS * b + s - 1)
                        tiles = [] if last and q == 3 else list(max_jobs_at(q, kt))
                        nb, qn = b + (q + 1) // QU, (q + 1) % QU
                        if kt == 0 and tiles:
                            pe.wait_ge(q_loaded[qn], 16 * (nb + 1))

                        slots = {2: (0, 2), 1: (1,)}.get(len(tiles), range(4))

                        def max_slot(i):
                            if i in slots and tiles:
                                n = tiles.pop(0)
                                max_tile(n, qn % 2, qn, 2 * b + (q + 1) // 2, nb, NMAX * (4 * b + q + 1) + n - 1)

                        max_slot(0)
                        for hq in range(4):
                            pair, j = hq // 2, hq % 2
                            mm = pe.matmul(score[s % 2][:, j, pair, :],
                                           stack[q % 2][64 * j:64 * j + ROWS, pair, kt * P:(kt + 1) * P],
                                           qs[64 * j:64 * j + ROWS, q, pair, :], start=True, stop=True)
                        mm.then_inc(scored, 1)
                        max_slot(1)
                    if s == TAIL:
                        pv(b, s - 1)
                    while count < len(plan) and plan[count][0] == s:
                        _, kind, u, i = plan[count]
                        need = {"M": 2 * (4 * b + u + 1), "X": 4 * b + u + 1, "W": 4 * b + 4}.get(kind)
                        job(NF + b * NJ + count, kind, b + u // QU, u, i, need)
                        count += 1
                    if s == TAIL:
                        break
                    max_slot(2)
                    if s >= 1:
                        pv(b, s - 1)
                    max_slot(3)

            all_batches(pe, body)

        @block.scalar
        def _(act):
            act.wait_ge(w_loaded, 16 * 12)

            def evacuate(count, kind, u, i, staged, pv_count):
                act.wait_ge(misc_ready, count + 1)
                if kind == "T":
                    act.activation(ctxT[:, :, i * 256:(i + 1) * 256], misc[:].rearrange("p (c n) -> p c n", c=DC),
                                   ACT.Copy).then_inc(misc_read, 1)
                elif kind == "K":
                    if i == 0 and staged is not None:
                        for h in range(2):
                            act.wait_ge(k_stacked[0][h], 16 * 12 * staged)
                            act.wait_ge(k_stacked[1][h], 16 * 12 * staged)
                    g = u % QU // 2
                    act.activation(k_hi[:, i * 512:(i + 1) * 512], misc[:], ACT.Identity, bias=bk_u[:, g:g + 1]).then_inc(khi_done, 1)
                elif kind == "V":
                    if pv_count is not None:
                        act.wait_ge(pv_done, pv_count)
                    act.activation(val[:, 2 * i:2 * i + 2, :, 0:DH],
                                   misc[:].rearrange("p (t h d) -> p t h d", t=2, h=H), ACT.Copy).then_inc(misc_read, 1)

            act.wait_ge(consts_set, 5)
            for n, (kind, u, i) in enumerate(FIRST_JOBS):
                if kind in "TKV":
                    evacuate(n, kind, u, i, None, None)

            def body(b, last):
                plan = misc_plan(last)
                count = 0
                for s in range(STEPS + 1):
                    if s < STEPS:
                        act.wait_ge(scored, STEPS * b + s + 1)
                        if s >= 2:
                            act.wait_ge(pv_done, STEPS * b + s - 1)
                        act.activation(prob[s % 2][:], score[s % 2][:], ACT.Exp).then_inc(exp_done, 1)
                    while count < len(plan) and plan[count][0] == s:
                        _, kind, u, i = plan[count]
                        if kind in "TKV":
                            evacuate(NF + b * NJ + count, kind, u, i, 2 * b + u // 2,
                                     STEPS * b + 3 * KT + 2 * i + 2)
                        count += 1

            all_batches(act, body)

        @block.vector
        def _(dve):
            dve.memset(stack[0][:].bitcast(F32), 1.0).then_inc(consts_set, 1)
            dve.memset(val[:, :, :, DH:DH + 1], 1.0).then_inc(consts_set, 1)
            dve.wait_ge(w_loaded, 16 * 12)
            dve.wait_ge(consts_set, 5)

            def max_read_tile(n, unit):
                chunk, pair, qh, j = max_job(n)
                dve.wait_ge(max_ready, NMAX * unit + n + 1)
                dve.tensor_reduce(max_parts[:, (2 * pair + j) * 2 + qh, chunk:chunk + 1], mx[j][:], AX.X, ALU.max)\
                    .then_inc(max_read, 1)

            def columns(unit):
                dve.wait_ge(max_read, NMAX * unit + NMAX)
                dve.tensor_reduce(neg_max[:], max_parts[:], AX.X, ALU.max, negate=True).then_inc(neg_found, 1)
                dve.wait_ge(neg_found, unit + 1)
                dve.tensor_copy(neg_hi[:], neg_max[:]).then_inc(neg_split, 1)
                dve.wait_ge(neg_split, unit + 1)
                hi = neg_hi[:].bitcast(F32).rearrange("p (h a) -> p h a", a=2)
                dve.tensor_copy(neg_cols[:, :, :, 0], hi).then_inc(neg_turnable, 1)
                dve.tensor_sub(neg_cols[:, :, :, 1], neg_max[:].rearrange("p (h a) -> p h a", a=2), hi)\
                    .then_inc(neg_turnable, 1)

            def evacuate(b, count, kind, u, i, first=False):
                if kind == "K":
                    g = u % QU // 2
                    dve.wait_ge(khi_done, 8 * (2 * b + u // 2) + i + 1)
                    dve.scalar_tensor_tensor(k_lo[:, i * 512:(i + 1) * 512], misc[:], bk_u[:, g:g + 1],
                                             k_hi[:, i * 512:(i + 1) * 512].bitcast(F32), ALU.add, ALU.subtract)\
                        .then_inc(misc_read, 1)
                elif kind == "M":
                    dve.wait_ge(misc_ready, count + 1)
                    if not first:
                        dve.wait_ge(neg_stacked, 16 * 8 * (4 * b + u))
                    dve.tensor_copy(neg_rows[:], misc[0:16, 0:P]).then_inc(misc_read, 1)
                elif kind == "X":
                    dve.wait_ge(misc_ready, count + 1)
                    dve.reciprocal(rden[:], misc[:, 0:NQ]).then_inc(misc_read, 1)
                    dve.wait_ge(misc_read, count + 1)
                    dve.tensor_mul(normed[:], head_out[:], rden[:]).then_inc(normed_done, 1)
                    dve.wait_ge(normed_done, 4 * b + u + 1)
                    dve.tensor_scalar(heads[:, u, :], normed[:], bv_u[:, u:u + 1], None, ALU.add)\
                        .then_inc(heads_done, 1)
                elif kind == "W":
                    dve.wait_ge(misc_ready, count + 1)
                    dve.wait_ge(res_loaded, 16 * (b + 1))
                    dve.wait_ge(x1_stored, 16 * (b + 1))
                    dve.tensor_add(x_out[:].rearrange("p i d -> p (i d)"), misc[:],
                                   x_res[:].rearrange("p i d -> p (i d)")).then_inc(misc_read, 1)

            def read_acc(b, q):
                dve.wait_ge(pv_done, STEPS * b + KT * (q + 1))
                for hq in range(4):
                    cp = dve.tensor_copy(head_out[32 * hq:32 * hq + DH + 1, :], acc[32 * hq:32 * hq + DH + 1, 0:NQ])
                cp.then_inc(acc_read, 1)

            for n, (kind, u, i) in enumerate(FIRST_JOBS):
                if kind == "V":
                    for m in range(4 * i, 4 * i + 4):
                        max_read_tile(m, 0)
                if kind == "M":
                    columns(0)
                if kind in "KM":
                    evacuate(0, n, kind, u, i, first=True)

            def body(b, last):
                plan = misc_plan(last)
                count = 0
                for s in range(STEPS + 1):
                    q, kt = s // KT, s % KT
                    if kt == 1 and q > 0:
                        read_acc(b, q - 1)
                    if s == TAIL:
                        read_acc(b, QU - 1)
                    if s < STEPS and not (last and q == 3):
                        for n in max_jobs_at(q, kt):
                            max_read_tile(n, 4 * b + q + 1)
                        if kt == MAX_STEPS:
                            columns(4 * b + q + 1)
                    while count < len(plan) and plan[count][0] == s:
                        _, kind, u, i = plan[count]
                        if kind in "KMXW":
                            evacuate(b, NF + b * NJ + count, kind, u, i)
                        count += 1

            all_batches(dve, body)


MAX_ROWS = 48
EXP_ROWS = 50
VD = 2 * DH
LAMBDA_INIT = 0.8 - 0.6 * math.exp(-0.3 * (4 - 1))
MASKED = -1e30


def project_stage(nc, x1, weights, v_w, parts, values):
    NT = NTOK // P
    with ExitStack() as ctx:
        def sb(name, shape, dt):
            return ctx.enter_context(nc.sbuf_tensor("p_" + name, shape, dt))

        def sem(name):
            return ctx.enter_context(nc.semaphore("p_" + name))

        x_in = sb("x_in", [P, NT, D], F32)
        xn = sb("xn", [P, NT, D], F32)
        xnT = sb("xnT", [P, DC, NTOK], F32)
        stats = sb("stats", [P, NT, 6], F32)
        mv = sb("mv", [P, NT, 2], F32)
        var_eps = sb("var_eps", [P, NT], F32)
        std = sb("std", [P, NT], F32)
        rstd = sb("rstd", [P, NT], F32)
        w = [sb(f"w{i}", [P, DC, D], F32) for i in range(4)]
        wv = sb("wv", [P, DC, 2 * D], F32)
        ident = sb("ident", [P, P], F32)
        hi = [sb(f"hi{i}", [P, 512], F32R) for i in range(2)]
        lo = [sb(f"lo{i}", [P, 512], F32R) for i in range(2)]
        vals = [sb(f"vals{i}", [P, H, VD + 1], F32) for i in range(2)]
        pt = [ctx.enter_context(nc.psum_tensor(f"p_pt{i}", [P, 512], F32)) for i in range(2)]
        pp = [ctx.enter_context(nc.psum_tensor(f"p_pp{i}", [P, 512], F32)) for i in range(2)]

        x_loaded, w_loaded, ident_set, ones_set = sem("x_loaded"), sem("w_loaded"), sem("ident_set"), sem("ones_set")
        stats_done, std_done, norm_done = sem("stats_done"), sem("std_done"), sem("norm_done")
        turned, turned_read = sem("turned"), sem("turned_read")
        projected, hi_done, lo_done = sem("projected"), sem("hi_done"), sem("lo_done")
        stored = [sem(f"stored{i}") for i in range(2)]
        v_done = sem("v_done")
        v_stored = [sem(f"v_stored{i}") for i in range(2)]
        NPJ = 16
        block = ctx.enter_context(nc.Block())

        @block.sync
        def _(sp):
            sp.dma_start(x_in[:], x1.rearrange("b (t p) d -> p (b t) d", p=P)).then_inc(x_loaded, 16)
            for i in range(4):
                sp.dma_start(w[i][:], weights[i].rearrange("(c p) n -> p c n", p=P)).then_inc(w_loaded, 16)
            sp.dma_start(wv[:], v_w.rearrange("(c p) n -> p c n", p=P)).then_inc(w_loaded, 16)
            for n in range(NPJ):
                i, g, half = n // 4, n // 2 % 2, n % 2
                sp.wait_ge(lo_done, n + 1)
                for part, tile in enumerate((hi, lo)):
                    sp.dma_start(parts[i, part, g * P:(g + 1) * P, half * 512:(half + 1) * 512],
                                 tile[n % 2][:].bitcast(F32)).then_inc(stored[n % 2], 16)
            for t in range(NT):
                sp.wait_ge(v_done, t + 1)
                sp.dma_start(values[t], vals[t % 2][:]).then_inc(v_stored[t % 2], 16)
            for i in range(2):
                sp.wait_ge(stored[i], 32 * NPJ // 2)
                sp.wait_ge(v_stored[i], 16 * NT // 2)

        @block.gpsimd
        def _(pool):
            pool.memset(ident[:], 0.0).then_inc(ident_set, 1)
            pool.wait_ge(ident_set, 1)
            pool.affine_select(out=ident[:], in_=ident[:], compare_op=ALU.not_equal, fill=1.0, base=0,
                               pattern=[[-1, P]], channel_multiplier=1).then_inc(ident_set, 1)
            for i in range(2):
                pool.memset(vals[i][:], 1.0).then_inc(ones_set, 1)

        @block.vector
        def _(dve):
            dve.wait_ge(x_loaded, 16)
            for t in range(NT):
                dve.bn_stats(stats[:, t, :], x_in[:, t, :]).then_inc(stats_done, 1)
            for t in range(NT):
                dve.wait_ge(stats_done, t + 1)
                dve.bn_aggr(mv[:, t, :], stats[:, t, :]).then_inc(stats_done, 1)
            dve.wait_ge(stats_done, 2 * NT)
            dve.tensor_scalar(var_eps[:], mv[:, :, 1], LN_EPS, None, ALU.add).then_inc(stats_done, 1)
            dve.wait_ge(std_done, 1)
            dve.reciprocal(rstd[:], std[:]).then_inc(stats_done, 1)
            dve.wait_ge(stats_done, 2 * NT + 2)
            for t in range(NT):
                dve.tensor_scalar(xn[:, t, :], x_in[:, t, :], mv[:, t, 0:1], rstd[:, t:t + 1],
                                  ALU.subtract, ALU.mult).then_inc(norm_done, 1)
            for n in range(NT // 4 * DC):
                c, t4 = n % DC, n // DC
                dve.wait_ge(turned, n + 1)
                dve.tensor_copy(xnT[:, c, t4 * 512:t4 * 512 + 512], pt[n % 2][:]).then_inc(turned_read, 1)
            for n in range(NPJ):
                dve.wait_ge(hi_done, n + 1)
                dve.scalar_tensor_tensor(lo[n % 2][:], pp[n % 2][:], DH ** -0.5 if n // 4 < 2 else 1.0,
                                         hi[n % 2][:].bitcast(F32), ALU.mult, ALU.subtract).then_inc(lo_done, 1)

        @block.tensor
        def _(pe):
            pe.wait_ge(ident_set, 2)
            for n in range(NT // 4 * DC):
                c, t4 = n % DC, n // DC
                pe.wait_ge(norm_done, 4 * t4 + 4)
                if n >= 2:
                    pe.wait_ge(turned_read, n - 1)
                for t in range(4):
                    mm = pe.transpose(pt[n % 2][:, t * P:(t + 1) * P], xn[:, 4 * t4 + t, c * P:(c + 1) * P], ident[:])
                mm.then_inc(turned, 1)
            pe.wait_ge(turned_read, NT // 4 * DC)
            pe.wait_ge(w_loaded, 80)
            for n in range(NPJ):
                i, g, half = n // 4, n // 2 % 2, n % 2
                if n >= 2:
                    pe.wait_ge(lo_done, n - 1)
                for c in range(DC):
                    mm = pe.matmul(pp[n % 2][:], w[i][:, c, g * P:(g + 1) * P],
                                   xnT[:, c, half * 512:half * 512 + 512], start=(c == 0), stop=(c == DC - 1))
                mm.then_inc(projected, 1)
            for t in range(NT):
                pe.wait_ge(*((lo_done, NPJ - 1 + t) if t < 2 else (v_done, t - 1)))
                for c in range(DC):
                    mm = pe.matmul(pp[t % 2][:], xnT[:, c, t * P:(t + 1) * P], wv[:, c, :],
                                   start=(c == 0), stop=(c == DC - 1))
                mm.then_inc(projected, 1)

        @block.scalar
        def _(act):
            act.wait_ge(stats_done, 2 * NT + 1)
            act.activation(std[:], var_eps[:], ACT.Sqrt).then_inc(std_done, 1)
            for n in range(NPJ):
                act.wait_ge(projected, n + 1)
                if n >= 2:
                    act.wait_ge(stored[n % 2], 32 * (n // 2))
                act.activation(hi[n % 2][:], pp[n % 2][:], ACT.Copy, scale=DH ** -0.5 if n // 4 < 2 else 1.0)\
                    .then_inc(hi_done, 1)
            act.wait_ge(ones_set, 2)
            for t in range(NT):
                act.wait_ge(projected, NPJ + t + 1)
                if t >= 2:
                    act.wait_ge(v_stored[t % 2], 16 * (t // 2))
                act.activation(vals[t % 2][:, :, 0:VD], pp[t % 2][:].rearrange("p (h d) -> p h d", h=H),
                               ACT.Copy).then_inc(v_done, 1)


def diff_stage(nc, parts, values, lambdas, neg_dram, y_all):
    NPAIR = H // 2
    with ExitStack() as ctx:
        def sb(name, shape, dt):
            return ctx.enter_context(nc.sbuf_tensor("d_" + name, shape, dt))

        def sem(name):
            return ctx.enter_context(nc.semaphore("d_" + name))

        def psum(name, shape):
            return ctx.enter_context(nc.psum_tensor("d_" + name, shape, F32))

        stack = [[sb(f"stack{b}{i}", [P, NPAIR, NQ], F32R) for i in range(4)] for b in range(2)]
        val = [sb(f"val{b}", [P, 2, H, VD + 1], F32) for b in range(2)]
        prob = [sb(f"prob{i}", [P, 2, 512], F32) for i in range(6)]
        ident_f = sb("ident_f", [P, P], F32)
        ident = sb("ident", [P, P], BF16)
        tri_f = sb("tri_f", [P, 2, P], F32)
        mask_q = [sb(f"mask_q{i}", [P, 512], BF16) for i in range(2)]
        mask_k = [sb(f"mask_k{i}", [P, 512], BF16) for i in range(2)]
        lam_in = sb("lam_in", [P, 4, D], F32)
        lam_prod = sb("lam_prod", [P, 2, D], F32)
        lam_sum = sb("lam_sum", [P, 2, H], F32)
        lam_exp = sb("lam_exp", [P, 2, H], F32)
        neg_lam = sb("neg_lam", [P, H], F32)
        neg_max = [sb(f"neg_max{b}", [P, 2, 2, 2, NPAIR], F32) for b in range(2)]
        neg_hi = [sb(f"neg_hi{b}", [P, 2, 2, 2, NPAIR], F32R) for b in range(2)]
        neg_cols = [sb(f"neg_cols{b}", [P, 2, 4, 2, NPAIR], F32) for b in range(2)]
        neg_rows = [sb(f"neg_rows{b}", [P, P], F32) for b in range(2)]
        rden = sb("rden", [P, 8], F32)
        scaled = sb("scaled", [P, 8, VD], F32)
        score = [psum(f"score{i}", [P, 2, 512]) for i in range(2)]
        mx = [psum(f"mx{i}", [P, 512]) for i in range(2)]
        y = [psum(f"y{i}", [P, 512]) for i in range(2)]

        zeroed, consts_set = sem("zeroed"), sem("consts_set")
        lam_loaded, lam_steps, lam_exped, lam_done = sem("lam_loaded"), sem("lam_steps"), sem("lam_exped"), sem("lam_done")
        loaded = [sem(f"loaded{b}") for b in range(2)]
        max_ready, max_read = sem("max_ready"), sem("max_read")
        split, cols_done, turned, rows_done = sem("split"), sem("cols_done"), sem("turned"), sem("rows_done")
        neg_out, neg_in = [sem(f"neg_out{b}") for b in range(2)], [sem(f"neg_in{b}") for b in range(2)]
        scored, exp_done, y_ready, y_step, y_read = sem("scored"), sem("exp_done"), sem("y_ready"), sem("y_step"), sem("y_read")
        NMAXJ = 24
        NG = 4
        block = ctx.enter_context(nc.Block())

        def max_jobs():
            jobs = [(0, m, 4 * p, 4, j) for m in range(2) for p in range(2) for j in range(2)]
            return jobs + [(1, m, 2 * p, 2, j) for m in range(2) for p in range(4) for j in range(2)]

        def batch_pairs(eng, body):
            with eng.Fori(0, B // 2) as i:
                body(i)

        @block.gpsimd
        def _(pool):
            for b in range(2):
                for i in (2, 3):
                    pool.memset(stack[b][i][:].bitcast(F32), 1.0).then_inc(consts_set, 1)
            pool.memset(ident_f[:], 0.0).then_inc(zeroed, 1)
            pool.memset(tri_f[:], 0.0).then_inc(zeroed, 1)
            pool.wait_ge(zeroed, 2)
            pool.affine_select(out=ident_f[:], in_=ident_f[:], compare_op=ALU.not_equal, fill=1.0, base=0,
                               pattern=[[-1, P]], channel_multiplier=1).then_inc(zeroed, 1)
            pool.affine_select(out=tri_f[:, 0, :], in_=tri_f[:, 0, :], compare_op=ALU.is_ge, fill=MASKED, base=0,
                               pattern=[[-1, P]], channel_multiplier=1).then_inc(zeroed, 1)
            pool.affine_select(out=tri_f[:, 1, :], in_=tri_f[:, 1, :], compare_op=ALU.is_ge, fill=MASKED, base=0,
                               pattern=[[1, P]], channel_multiplier=-1).then_inc(zeroed, 1)

        @block.sync
        def _(sp):
            for i in range(4):
                sp.dma_start(lam_in[:, i, :], lambdas[i].rearrange("(o h) d -> o (h d)", o=1).broadcast_to([P, D]))\
                    .then_inc(lam_loaded, 16)
            sp.wait_ge(consts_set, 4)

            def load(b, par):
                for i in range(4):
                    for j in range(2):
                        for r, part in enumerate((0, 0, 1) if i < 2 else (0, 1, 0)):
                            sp.dma_start(stack[par][i][64 * j + 16 * r:64 * j + 16 * r + DH, :, :].bitcast(F32),
                                         parts[i, part, :, b, :].rearrange("(n j d) t -> j d n t", j=2, d=DH)[j])\
                                .then_inc(loaded[par], 16)
                sp.dma_start(val[par][:], values[b].rearrange("t p h v -> p t h v"))\
                    .then_inc(loaded[par], 16)

            def spread(par, count):
                sp.wait_ge(rows_done, count)
                for qh in range(2):
                    sp.dma_start(neg_dram[par, :, qh * P:(qh + 1) * P], neg_rows[par][64 * qh:64 * qh + 64, :])\
                        .then_inc(neg_out[par], 16)

            def gather(par, count):
                sp.wait_ge(neg_out[par], count)
                for m in range(2):
                    for j in range(2):
                        sp.dma_start(stack[par][m][64 * j + 48:64 * j + 50, :, :].bitcast(F32),
                                     neg_dram[par, 16 * (2 * m + j):16 * (2 * m + j) + 16, :]
                                     .rearrange("(r n) q -> r n q", r=2)).then_inc(neg_in[par], 16)

            load(0, 0)
            load(1, 1)

            def body(i, more):
                for par in range(2):
                    spread(par, 2 * i + par + 1)
                    gather(par, 32 * (i + 1))
                if more:
                    for par in range(2):
                        sp.wait_ge(y_ready, 8 * (2 * i + par) + 8)
                        load(2 * i + par + 2, par)

            for i in range(B // 2):
                body(i, i < B // 2 - 1)

        @block.tensor
        def _(pe):
            pe.wait_ge(consts_set, 10)

            def max_pass(i, par):
                pe.wait_ge(loaded[par], 16 * 25 * (i + 1))
                for n, (qh, m, p0, np_, j) in enumerate(max_jobs()):
                    pe.wait_ge(max_read, NMAXJ * (2 * i + par) + n + 1)
                    pe.matmul(mx[j][:], ident[:], mask_q[qh][:], start=True, stop=False)
                    nk = P * (qh + 1)
                    for p in range(np_):
                        mm = pe.matmul(mx[j][:, p * nk:(p + 1) * nk],
                                       stack[par][m][64 * j:64 * j + MAX_ROWS, p0 + p, qh * P:(qh + 1) * P],
                                       stack[par][2 + m][64 * j:64 * j + MAX_ROWS, p0 + p, 0:nk],
                                       start=False, stop=(p == np_ - 1))
                    mm.then_inc(max_ready, 1)

            def turn(i, par):
                pe.wait_ge(cols_done, 2 * (2 * i + par) + 2)
                if par == 0:
                    pe.wait_ge(y_read, 16 * i + 2)
                else:
                    pe.wait_ge(rows_done, 2 * i + 1)
                pe.transpose(y[0][:, 0:P], neg_cols[par][:].rearrange("p a m r n -> p (a m r n)"), ident_f[:])\
                    .then_inc(turned, 1)

            def exp_scores(i, par, n):
                g, k = n // 3, n % 3
                pe.wait_ge(exp_done, 12 * (2 * i + par) + n + 1)
                s = score[n % 2]
                for j in range(2):
                    pe.matmul(s[:, j, :], ident[:], mask_k[k // 2][:], start=True, stop=False)
                for pl in range(2):
                    for m in ((k,) if k < 2 else (0, 1)):
                        for j in range(2):
                            out = s[:, j, pl * NQ:(pl + 1) * NQ] if k < 2 else s[:, j, (2 * m + pl) * P:(2 * m + pl + 1) * P]
                            q0, k0 = (0, 0) if k < 2 else (P, P)
                            mm = pe.matmul(out, stack[par][2 + m][64 * j:64 * j + EXP_ROWS, 2 * g + pl, k0:k0 + P],
                                           stack[par][m][64 * j:64 * j + EXP_ROWS, 2 * g + pl, q0:NQ],
                                           start=False, stop=(pl == 1 and m == (k if k < 2 else 1)))
                mm.then_inc(scored, 1)

            def outputs(i, par, g):
                pe.wait_ge(exp_done, 12 * (2 * i + par) + 3 * g + 3 + 2)
                a = [prob[(3 * g + k) % 6] for k in range(3)]
                for qh in range(2):
                    pe.wait_ge(y_read, 8 * (2 * i + par) + 2 * g + qh + 1)
                    for m in range(2):
                        for hl in range(4):
                            j, pl, h = hl % 2, hl // 2, 4 * g + hl
                            out = y[qh][:, (4 * m + hl) * (VD + 1):(4 * m + hl + 1) * (VD + 1)]
                            mm = pe.matmul(out, a[m][:, j, pl * NQ + qh * P:pl * NQ + (qh + 1) * P],
                                           val[par][:, 0, h, :], start=True, stop=(qh == 0))
                            if qh == 1:
                                mm = pe.matmul(out, a[2][:, j, (2 * m + pl) * P:(2 * m + pl + 1) * P],
                                               val[par][:, 1, h, :], start=False, stop=True)
                    mm.then_inc(y_ready, 1)

            def body(i):
                for par in range(2):
                    max_pass(i, par)
                    turn(i, par)
                for par in range(2):
                    pe.wait_ge(neg_in[par], 64 * (i + 1))
                    for n in range(3 * NG + 3):
                        if n < 3 * NG:
                            exp_scores(i, par, n)
                        if n >= 3 and n % 3 == 2:
                            outputs(i, par, n // 3 - 1)

            batch_pairs(pe, body)

        @block.scalar
        def _(act):
            act.sem_inc(exp_done, 2)
            act.wait_ge(lam_steps, 4)
            act.activation(lam_exp[:], lam_sum[:], ACT.Exp).then_inc(lam_exped, 1)

            def body(i):
                for par in range(2):
                    act.wait_ge(turned, 2 * i + par + 1)
                    act.activation(neg_rows[par][:], y[0][:, 0:P], ACT.Copy).then_inc(rows_done, 1)
                for par in range(2):
                    for n in range(3 * NG):
                        act.wait_ge(scored, 12 * (2 * i + par) + n + 1)
                        act.activation(prob[n % 6][:], score[n % 2][:], ACT.Exp).then_inc(exp_done, 1)

            batch_pairs(act, body)

        @block.vector
        def _(dve):
            dve.sem_inc(max_read, 2)
            dve.sem_inc(y_read, 2)
            dve.wait_ge(zeroed, 5)
            dve.tensor_copy(ident[:], ident_f[:]).then_inc(consts_set, 1)
            for i in range(2):
                dve.memset(mask_q[i][:], 0.0).then_inc(lam_done, 1)
                dve.memset(mask_k[i][:], 0.0).then_inc(lam_done, 1)
            dve.wait_ge(lam_done, 4)
            for blocks, dst, kind in ((range(4), mask_q[0], 0), ((1, 3), mask_q[1], 0),
                                      ((0, 2), mask_k[0], 1), (range(4), mask_k[1], 1)):
                for k in blocks:
                    cp = dve.tensor_copy(dst[:, k * P:(k + 1) * P], tri_f[:, kind, :])
                cp.then_inc(consts_set, 1)
            dve.sem_inc(consts_set, 1)
            dve.wait_ge(lam_loaded, 64)
            for i in range(2):
                dve.tensor_mul(lam_prod[:, i, :], lam_in[:, 2 * i, :], lam_in[:, 2 * i + 1, :]).then_inc(lam_steps, 1)
            dve.wait_ge(lam_steps, 2)
            for i in range(2):
                dve.tensor_reduce(lam_sum[:, i, :], lam_prod[:, i, :].rearrange("p (h d) -> p h d", h=H), AX.X, ALU.add)\
                    .then_inc(lam_steps, 1)
            dve.wait_ge(lam_exped, 1)
            dve.scalar_tensor_tensor(neg_lam[:], lam_exp[:, 1, :], LAMBDA_INIT, lam_exp[:, 0, :],
                                     ALU.subtract, ALU.subtract).then_inc(lam_done, 1)
            dve.wait_ge(lam_done, 5)

            def max_pass(i, par):
                nb = 2 * i + par
                for n, (qh, m, p0, np_, j) in enumerate(max_jobs()):
                    dve.wait_ge(max_ready, NMAXJ * nb + n + 1)
                    dve.tensor_reduce(neg_max[par][:, qh, m, j, p0:p0 + np_],
                                      mx[j][:].rearrange("p (n k) -> p n k", n=np_), AX.X, ALU.max, negate=True)\
                        .then_inc(max_read, 1)
                dve.wait_ge(max_read, NMAXJ * nb + NMAXJ + 2)
                dve.tensor_copy(neg_hi[par][:], neg_max[par][:]).then_inc(split, 1)
                dve.wait_ge(split, nb + 1)
                hi = neg_hi[par][:].bitcast(F32).rearrange("p a m j n -> p a (m j) n")
                full = neg_max[par][:].rearrange("p a m j n -> p a (m j) n")
                dve.tensor_copy(neg_cols[par][:, :, :, 0, :], hi).then_inc(cols_done, 1)
                dve.tensor_sub(neg_cols[par][:, :, :, 1, :], full, hi).then_inc(cols_done, 1)

            def body(i):
                for par in range(2):
                    max_pass(i, par)
                for par in range(2):
                    for g in range(NG):
                        for qh in range(2):
                            nb = 8 * (2 * i + par) + 2 * g + qh
                            dve.wait_ge(y_ready, nb + 1)
                            yv = y[qh][:, 0:8 * (VD + 1)].rearrange("p (n v) -> p n v", n=8)
                            dve.reciprocal(rden[:], yv[:, :, VD]).then_inc(y_step, 1)
                            dve.wait_ge(y_step, 3 * nb + 1)
                            dve.tensor_mul(rden[:, 4:8], rden[:, 4:8], neg_lam[:, 4 * g:4 * g + 4]).then_inc(y_step, 1)
                            dve.wait_ge(y_step, 3 * nb + 2)
                            dve.tensor_mul(scaled[:], yv[:, :, 0:VD], rden[:].unsqueeze(2).broadcast_to([P, 8, VD]))\
                                .then_inc(y_read, 1)
                            dve.wait_ge(y_read, nb + 3)
                            dve.tensor_add(y_all[:, 2 * (2 * i + par) + qh, 4 * g:4 * g + 4, :], scaled[:, 0:4, :],
                                           scaled[:, 4:8, :]).then_inc(y_step, 1)
                            dve.wait_ge(y_step, 3 * nb + 3)

            batch_pairs(dve, body)


def output_stage(nc, x1, c_w, y_all, x2, xn2):
    NT = NTOK // P
    YC = 2 * D // P
    with ExitStack() as ctx:
        def sb(name, shape, dt):
            return ctx.enter_context(nc.sbuf_tensor("o_" + name, shape, dt))

        def sem(name):
            return ctx.enter_context(nc.semaphore("o_" + name))

        x_in = sb("x_in", [P, NT, D], F32)
        x_out = sb("x_out", [P, NT, D], F32)
        xn = sb("xn", [P, NT, D], F32)
        w = sb("w", [P, YC, D], F32)
        ident = sb("ident", [P, P], F32)
        mean = sb("mean", [P, NT, H], F32)
        neg_mean = sb("neg_mean", [P, NT, H], F32)
        square = sb("square", [P, 2, 2 * D], F32)
        ssum = sb("ssum", [P, NT, H], F32)
        var = sb("var", [P, NT, H], F32)
        std = sb("std", [P, NT, H], F32)
        rstd = sb("rstd", [P, NT, H], F32)
        yn = sb("yn", [P, NT, 2 * D], F32)
        ynT = sb("ynT", [P, 2, YC, P], F32)
        stats = sb("stats", [P, NT, 6], F32)
        mv = sb("mv", [P, NT, 2], F32)
        var_x = sb("var_x", [P, NT], F32)
        std_x = sb("std_x", [P, NT], F32)
        rstd_x = sb("rstd_x", [P, NT], F32)
        pt = [ctx.enter_context(nc.psum_tensor(f"o_pt{i}", [P, 512], F32)) for i in range(2)]
        po = [ctx.enter_context(nc.psum_tensor(f"o_po{i}", [P, 512], F32)) for i in range(2)]
        loaded, ident_set = sem("loaded"), sem("ident_set")
        chain, std_done, normed, turned, turned_read = sem("chain"), sem("std_done"), sem("normed"), sem("turned"), sem("turned_read")
        projected, x_done, stat_done, stdx_done, xn_done, stored = (sem("projected"), sem("x_done"), sem("stat_done"),
                                                                    sem("stdx_done"), sem("xn_done"), sem("stored"))
        block = ctx.enter_context(nc.Block())

        def y3(t):
            return y_all[:, t, :, :]

        def each(ap):
            return ap.unsqueeze(2).broadcast_to([P, H, VD])

        @block.sync
        def _(sp):
            sp.dma_start(w[:], c_w.rearrange("(c p) n -> p c n", p=P)).then_inc(loaded, 16)
            sp.dma_start(x_in[:], x1.rearrange("b (t p) d -> p (b t) d", p=P)).then_inc(loaded, 16)
            for t in range(NT):
                sp.wait_ge(x_done, t + 1)
                sp.dma_start(x2[t * P:(t + 1) * P, :], x_out[:, t, :]).then_inc(stored, 16)
            for t in range(NT):
                sp.wait_ge(xn_done, t + 1)
                sp.dma_start(xn2[t * P:(t + 1) * P, :], xn[:, t, :]).then_inc(stored, 16)
            sp.wait_ge(stored, 32 * NT)

        @block.gpsimd
        def _(pool):
            pool.memset(ident[:], 0.0).then_inc(ident_set, 1)
            pool.wait_ge(ident_set, 1)
            pool.affine_select(out=ident[:], in_=ident[:], compare_op=ALU.not_equal, fill=1.0, base=0,
                               pattern=[[-1, P]], channel_multiplier=1).then_inc(ident_set, 1)

        @block.vector
        def _(dve):
            c = [0]

            def link(ins):
                c[0] += 1
                ins.then_inc(chain, 1)
                dve.wait_ge(chain, c[0])

            for t in range(NT):
                link(dve.tensor_reduce(mean[:, t, :], y3(t), AX.X, ALU.add))
            link(dve.tensor_scalar(neg_mean[:], mean[:], -1.0 / VD, None, ALU.mult))
            for t in range(NT):
                link(dve.tensor_add(y3(t), y3(t), each(neg_mean[:, t, :])))
                s = square[:, t % 2, :].rearrange("p (h v) -> p h v", h=H)
                link(dve.tensor_mul(s, y3(t), y3(t)))
                link(dve.tensor_reduce(ssum[:, t, :], s, AX.X, ALU.add))
            link(dve.tensor_scalar(var[:], ssum[:], 1.0 / VD, LN_EPS, ALU.mult, ALU.add))
            dve.wait_ge(std_done, 1)
            link(dve.reciprocal(rstd[:], std[:]))
            link(dve.tensor_scalar(var[:], rstd[:], 1.0 - LAMBDA_INIT, None, ALU.mult))
            for t in range(NT):
                dve.tensor_mul(yn[:, t, :].rearrange("p (h v) -> p h v", h=H), y3(t), each(var[:, t, :]))\
                    .then_inc(normed, 1)
            dve.wait_ge(loaded, 32)
            for t in range(NT):
                dve.wait_ge(turned, t + 1)
                dve.tensor_copy(ynT[:, t % 2, :, :].rearrange("p c n -> p (c n)"), pt[t % 2][:]).then_inc(turned_read, 1)
                dve.wait_ge(projected, t + 1)
                dve.tensor_add(x_out[:, t, :], po[t % 2][:, 0:D], x_in[:, t, :]).then_inc(x_done, 1)
                dve.wait_ge(x_done, t + 1)
                dve.bn_stats(stats[:, t, :], x_out[:, t, :]).then_inc(stat_done, 1)
                dve.wait_ge(stat_done, 2 * t + 1)
                dve.bn_aggr(mv[:, t, :], stats[:, t, :]).then_inc(stat_done, 1)
            dve.wait_ge(stat_done, 2 * NT)
            dve.tensor_scalar(var_x[:], mv[:, :, 1], LN_EPS, None, ALU.add).then_inc(stat_done, 1)
            dve.wait_ge(stdx_done, 1)
            link(dve.reciprocal(rstd_x[:], std_x[:]))
            for t in range(NT):
                dve.tensor_scalar(xn[:, t, :], x_out[:, t, :], mv[:, t, 0:1], rstd_x[:, t:t + 1],
                                  ALU.subtract, ALU.mult).then_inc(xn_done, 1)

        @block.scalar
        def _(act):
            act.wait_ge(chain, 4 * NT + 2)
            act.activation(std[:], var[:], ACT.Sqrt).then_inc(std_done, 1)
            act.wait_ge(stat_done, 2 * NT + 1)
            act.activation(std_x[:], var_x[:], ACT.Sqrt).then_inc(stdx_done, 1)

        @block.tensor
        def _(pe):
            pe.wait_ge(ident_set, 2)
            pe.wait_ge(loaded, 32)

            def turn(t):
                pe.wait_ge(normed, t + 1)
                if t >= 2:
                    pe.wait_ge(turned_read, t - 1)
                for c in range(YC):
                    mm = pe.transpose(pt[t % 2][:, c * P:(c + 1) * P], yn[:, t, c * P:(c + 1) * P], ident[:])
                mm.then_inc(turned, 1)

            turn(0)
            for t in range(NT):
                if t + 1 < NT:
                    turn(t + 1)
                pe.wait_ge(turned_read, t + 1)
                if t >= 2:
                    pe.wait_ge(x_done, t - 1)
                for c in range(YC):
                    mm = pe.matmul(po[t % 2][:, 0:D], ynT[:, t % 2, c, :], w[:, c, :], start=(c == 0), stop=(c == YC - 1))
                mm.then_inc(projected, 1)


E = 8
CAP = 512
FF = 1024
NW = 2048
ST = CAP // P
FC = FF // P


def moe_stage(nc, x2, xn2, combine_weights, top_idx, W1, b1, W2, b2, out):
    NT = NTOK // P
    with ExitStack() as ctx:
        def sb(name, shape, dt):
            return ctx.enter_context(nc.sbuf_tensor("e_" + name, shape, dt))

        def sem(name):
            return ctx.enter_context(nc.semaphore("e_" + name))

        def psum(name, shape):
            return ctx.enter_context(nc.psum_tensor("e_" + name, shape, F32))

        idx = sb("idx", [P, ST, E], I32)
        idx_clamped = sb("idx_clamped", [P, ST, E], I32)
        idx_f = sb("idx_f", [P, E, ST], F32)
        iota_i = sb("iota_i", [P, NTOK], I32)
        iota = sb("iota", [P, NTOK], F32)
        weight_rows = sb("weight_rows", [P, E, ST, E], F32)
        weight = [sb(f"weight{i}", [P, ST], F32) for i in range(2)]
        ident = sb("ident", [P, P], F32)
        zeros = sb("zeros", [1, 512], BF16)
        b1_rows = sb("b1_rows", [P, P], F32)
        b1_cols = sb("b1_cols", [P, P], F32)
        b2_all = sb("b2_all", [P, E, D], F32)
        w1 = [sb(f"w1_{i}", [P, DC, FF], F32) for i in range(2)]
        w2 = [sb(f"w2_{i}", [P, FC, D], F32) for i in range(2)]
        g = [sb(f"g{i}", [P, ST, D], F32) for i in range(2)]
        gT = sb("gT", [P, DC, CAP], F32)
        h = sb("h", [P, FC, CAP], F32)
        biased = sb("biased", [P, 2, D], F32)
        v_hi = sb("v_hi", [P, 2, D], F32R)
        v_lo = sb("v_lo", [P, 2, D], F32R)
        onehot = sb("onehot", [P, 2, NTOK], F32R)
        x_in = sb("x_in", [P, NT, D], F32)
        x_out = sb("x_out", [P, NT, D], F32)
        ph = [psum(f"ph{i}", [P, CAP]) for i in range(2)]
        shared = [psum(f"shared{i}", [P, CAP]) for i in range(2)]
        pt = shared[1]
        po = [shared[i][:, 0:D] for i in (0, 1, 0, 0)]
        acc = psum("acc", [P, NT, D])

        idx_loaded, b_loaded, x_loaded = sem("idx_loaded"), sem("b_loaded"), sem("x_loaded")
        w_loaded = [sem(f"w_loaded{i}") for i in range(2)]
        gathered = [sem(f"gathered{i}") for i in range(2)]
        weights_in = [sem(f"weights_in{i}") for i in range(2)]
        ident_set, iota_set, consts_set, idx_set = sem("ident_set"), sem("iota_set"), sem("consts_set"), sem("idx_set")
        b1_turned, b1_done = sem("b1_turned"), sem("b1_done")
        turned, gT_done = sem("turned"), sem("gT_done")
        hidden, gelu_done = sem("hidden"), sem("gelu_done")
        experted, bias_done, hi_done, v_done = sem("experted"), sem("bias_done"), sem("hi_done"), sem("v_done")
        weight_set, onehot_set, scattered = sem("weight_set"), sem("onehot_set"), sem("scattered")
        summed, stored = sem("summed"), sem("stored")
        block = ctx.enter_context(nc.Block())

        def expert_pairs(eng, body):
            with eng.Fori(0, E // 2 - 1) as i:
                body(i, True)
            body(E // 2 - 1, False)

        @block.sync
        def _(sp):
            sp.dma_start(idx[:], top_idx.rearrange("(p t) e -> p t e", t=ST)).then_inc(idx_loaded, 16)
            sp.wait_ge(consts_set, 1)
            sp.dma_start(b1_rows[0:E * FC, :], b1.rearrange("e (f p) -> (e f) p", p=P)).then_inc(b_loaded, 16)

            def load(n, par):
                sp.dma_start(w1[par][:], W1[n].rearrange("(c p) f -> p c f", p=P)).then_inc(w_loaded[par], 16)
                sp.dma_start(w2[par][:], W2[n].rearrange("(f p) d -> p f d", p=P)).then_inc(w_loaded[par], 16)

            load(0, 0)
            load(1, 1)
            sp.dma_start(b2_all[:], b2.rearrange("(o e) d -> o e d", o=1).broadcast_to([P, E, D])).then_inc(b_loaded, 16)
            sp.dma_start(x_in[:], x2.rearrange("(t p) d -> p t d", p=P)).then_inc(x_loaded, 16)
            with sp.Fori(0, E // 2 - 1) as i:
                for par in range(2):
                    sp.wait_ge(experted, ST * (2 * i + par) + ST)
                    load(2 * i + par + 2, par)
            for t in range(NT):
                sp.wait_ge(summed, t + 1)
                sp.dma_start(out[t * P:(t + 1) * P, :], x_out[:, t, :]).then_inc(stored, 16)
            sp.wait_ge(stored, 16 * NT)

        @block.gpsimd
        def _(pool):
            pool.memset(ident[:], 0.0).then_inc(ident_set, 1)
            pool.iota(iota_i[:], pattern=[[1, NTOK]], base=0, channel_multiplier=0).then_inc(iota_set, 1)
            pool.wait_ge(ident_set, 1)
            pool.affine_select(out=ident[:], in_=ident[:], compare_op=ALU.not_equal, fill=1.0, base=0,
                               pattern=[[-1, P]], channel_multiplier=1).then_inc(ident_set, 1)
            pool.wait_ge(idx_set, 1)
            for n in range(E):
                par = n % 2
                if n >= 2:
                    pool.wait_ge(turned, DC * (n - 1))
                    pool.wait_ge(weight_set, n - 1)
                for t in range(ST):
                    pool.indirect_dma_start(g[par][:, t, :], None, xn2,
                                            bass.IndirectOffsetOnAxis(ap=idx_clamped[:, t, n:n + 1], axis=0))\
                        .then_inc(gathered[par], 16)
                for t in range(ST):
                    pool.indirect_dma_start(weight_rows[:, n, t, :], None, combine_weights,
                                            bass.IndirectOffsetOnAxis(ap=idx[:, t, n:n + 1], axis=0))\
                        .then_inc(weights_in[par], 16)

        @block.tensor
        def _(pe):
            pe.wait_ge(consts_set, 2)
            for k in range(NT // 2):
                pe.matmul(acc[:, 2 * k:2 * k + 2, :], zeros[0:1, 0:P], zeros[0:1, :], start=True, stop=False)
            pe.wait_ge(ident_set, 2)
            pe.wait_ge(b_loaded, 32)
            pe.transpose(shared[0][:, 0:P], b1_rows[:], ident[:]).then_inc(b1_turned, 1)
            pe.wait_ge(b1_done, 1)

            def turn(n, i, par, c):
                if c == 0:
                    pe.wait_ge(gathered[par], 16 * ST * (i + 1))
                else:
                    pe.wait_ge(gT_done, DC * n + c)
                for t in range(ST):
                    mm = pe.transpose(pt[:, t * P:(t + 1) * P], g[par][:, t, c * P:(c + 1) * P], ident[:])
                mm.then_inc(turned, 1)

            def scatter(n, t):
                pe.wait_ge(v_done, ST * n + t + 1)
                pe.wait_ge(onehot_set, ST * n + t + 1)
                for k in range(NT):
                    for v in (v_hi, v_lo):
                        mm = pe.matmul(acc[:, k, :], onehot[:, t % 2, k * P:(k + 1) * P], v[:, t % 2, :],
                                       start=False, stop=False)
                mm.then_inc(scattered, 1)

            def body(i, more):
                for par in range(2):
                    n = 2 * i + par
                    pe.wait_ge(w_loaded[par], 32 * (i + 1))
                    pe.wait_ge(gT_done, DC * n + DC)
                    for f in range(FC):
                        pe.wait_ge(gelu_done, FC * n + f + 1)
                        for c in range(DC):
                            mm = pe.matmul(ph[f % 2][:], w1[par][:, c, f * P:(f + 1) * P], gT[:, c, :],
                                           start=(c == 0), stop=(c == DC - 1))
                        mm.then_inc(hidden, 1)
                    pe.wait_ge(gelu_done, FC * n + FC + 2)
                    for t in range(ST):
                        pe.wait_ge(bias_done, ST * n + (0, 0, 1, 3)[t] + 1)
                        for f in range(FC):
                            mm = pe.matmul(po[t], h[:, f, t * P:(t + 1) * P], w2[par][:, f, :],
                                           start=(f == 0), stop=(f == FC - 1))
                        mm.then_inc(experted, 1)
                        if t == 3 and (more or par == 0):
                            turn(n + 1, i + par, 1 - par, 1)
                        if t >= 1:
                            scatter(n, t - 1)
                        if t == 2 and (more or par == 0):
                            pe.wait_ge(bias_done, ST * n + 1 + 2)
                            turn(n + 1, i + par, 1 - par, 0)
                    scatter(n, ST - 1)

            turn(0, 0, 0, 0)
            turn(0, 0, 0, 1)
            expert_pairs(pe, body)
            for k in range(NT // 2):
                mm = pe.matmul(acc[:, 2 * k:2 * k + 2, :], zeros[0:1, 0:P], zeros[0:1, :], start=False, stop=True)
            mm.then_inc(scattered, 1)

        @block.scalar
        def _(act):
            act.sem_inc(gelu_done, 2)
            act.wait_ge(b1_turned, 1)
            act.activation(b1_cols[:], shared[0][:, 0:P], ACT.Copy).then_inc(b1_done, 1)
            act.wait_ge(b1_done, 1)

            def rows(n):
                for c in range(DC):
                    act.wait_ge(turned, DC * n + c + 1)
                    act.activation(gT[:, c, :], pt[:], ACT.Copy).then_inc(gT_done, 1)

            def body(i, more):
                for par in range(2):
                    n = 2 * i + par
                    for f in range(FC):
                        act.wait_ge(hidden, FC * n + f + 1)
                        act.activation(h[:, f, :], ph[f % 2][:], ACT.Gelu_apprx_tanh,
                                       bias=b1_cols[:, bass.ds(FC * n + f, 1)]).then_inc(gelu_done, 1)
                    if more or par == 0:
                        rows(n + 1)

            rows(0)
            expert_pairs(act, body)

        @block.vector
        def _(dve):
            dve.sem_inc(bias_done, 1)
            dve.sem_inc(scattered, 2)
            dve.memset(b1_rows[:], 0.0).then_inc(consts_set, 1)
            dve.memset(zeros[:], 0.0).then_inc(consts_set, 1)
            dve.wait_ge(idx_loaded, 16)
            dve.tensor_scalar(idx_clamped[:], idx[:], NTOK - 1, None, ALU.min).then_inc(idx_set, 1)
            dve.tensor_copy(idx_f[:], idx[:].rearrange("p t e -> p e t")).then_inc(idx_set, 1)
            dve.wait_ge(iota_set, 1)
            dve.tensor_copy(iota[:], iota_i[:]).then_inc(iota_set, 1)
            dve.wait_ge(iota_set, 2)
            dve.wait_ge(idx_set, 2)
            dve.wait_ge(b_loaded, 32)

            def body(i, more):
                for par in range(2):
                    n = 2 * i + par
                    dve.wait_ge(weights_in[par], 16 * ST * (i + 1))
                    dve.tensor_copy(weight[par][:], weight_rows[:, bass.ds(n, 1), :, bass.ds(n, 1)]).then_inc(weight_set, 1)
                    dve.wait_ge(weight_set, n + 1)
                    for t in range(ST):
                        dve.wait_ge(scattered, ST * n + t + 1)
                        dve.tensor_scalar(onehot[:, t % 2, :], iota[:], idx_f[:, bass.ds(n, 1), t], None, ALU.is_equal)\
                            .then_inc(onehot_set, 1)
                        dve.wait_ge(experted, ST * n + t + 1)
                        dve.tensor_add(biased[:, t % 2, :], po[t], b2_all[:, bass.ds(n, 1), :])\
                            .then_inc(bias_done, 1)
                        dve.wait_ge(bias_done, ST * n + t + 2)
                        dve.tensor_scalar(v_hi[:, t % 2, :], biased[:, t % 2, :], weight[par][:, t:t + 1], None, ALU.mult)\
                            .then_inc(hi_done, 1)
                        dve.wait_ge(hi_done, ST * n + t + 1)
                        dve.scalar_tensor_tensor(v_lo[:, t % 2, :], biased[:, t % 2, :], weight[par][:, t:t + 1],
                                                 v_hi[:, t % 2, :].bitcast(F32), ALU.mult, ALU.subtract).then_inc(v_done, 1)

            expert_pairs(dve, body)
            dve.wait_ge(scattered, ST * E + 3)
            dve.wait_ge(x_loaded, 16)
            for t in range(NT):
                dve.tensor_add(x_out[:, t, :], acc[:, t, :], x_in[:, t, :]).then_inc(summed, 1)


_INS = ["x", "ctx_1024", "mask_Bx1x1xS2_ik0", "L0_xattn_Wq", "L0_xattn_bq", "L0_xattn_Wk", "L0_xattn_bk",
        "L0_xattn_Wv", "L0_xattn_bv", "L0_xattn_Wo", "L0_xattn_bo",
        "L0_attn_q1_w", "L0_attn_q2_w", "L0_attn_k1_w", "L0_attn_k2_w", "L0_attn_v_w", "L0_attn_c_w",
        "L0_attn_lambda_q1", "L0_attn_lambda_k1", "L0_attn_lambda_q2", "L0_attn_lambda_k2",
        "L0_ffn_combine_weights", "L0_ffn_top_idx", "L0_ffn_W1", "L0_ffn_b1", "L0_ffn_W2", "L0_ffn_b2"]


def kernel(**inputs):
    import numpy as _np
    import concourse.bacc as _bacc
    from concourse import mybir as _mybir
    from concourse.bass_utils import run_bass_kernel_spmd as _run

    nc = _bacc.Bacc("TRN2", target_bir_lowering=False, num_devices=1)
    arrays, t = {}, {}
    for name in _INS:
        a = _np.ascontiguousarray(inputs[name])
        arrays[f"in_{name}"] = a
        t[name] = nc.dram_tensor(f"in_{name}", a.shape, _mybir.dt.from_np(a.dtype), kind="ExternalInput").ap()
    out = nc.dram_tensor("out_0", (B, NQ, D), F32, kind="ExternalOutput").ap()
    build(nc, t, out)
    r = _run(nc, [arrays], core_ids=[0])
    return r.results[0]["out_0"]


def cross_attention(nc, t, x1):
    q_stacks = nc.dram_tensor("q_stacks", (B, QU, P, 2, NQ), F32, kind="Internal").ap()
    mask_rows = nc.dram_tensor("mask_rows", (2, B, NK), F32, kind="Internal").ap()
    query_stage(nc, t["x"], t["L0_xattn_Wq"], t["L0_xattn_bq"], t["mask_Bx1x1xS2_ik0"], q_stacks, mask_rows)
    cross_stage(nc, t["x"], t["ctx_1024"], t["L0_xattn_Wk"], t["L0_xattn_bk"], t["L0_xattn_Wv"], t["L0_xattn_bv"],
                t["L0_xattn_Wo"], t["L0_xattn_bo"], q_stacks, mask_rows, x1)


def self_attention(nc, t, x1, x2, xn2):
    parts = nc.dram_tensor("attn_parts", (4, 2, D, NTOK), F32, kind="Internal").ap()
    values = nc.dram_tensor("attn_values", (NTOK // P, P, H, VD + 1), F32, kind="Internal").ap()
    neg_dram = nc.dram_tensor("attn_neg", (2, 64, NQ), F32, kind="Internal").ap()
    names = ("L0_attn_q1_w", "L0_attn_q2_w", "L0_attn_k1_w", "L0_attn_k2_w")
    project_stage(nc, x1, [t[n] for n in names], t["L0_attn_v_w"], parts, values)
    lambdas = [t["L0_attn_lambda_" + n] for n in ("q1", "k1", "q2", "k2")]
    with nc.sbuf_tensor("y_all", [P, NTOK // P, H, VD], F32) as y_all:
        diff_stage(nc, parts.rearrange("i r n (b t) -> i r n b t", b=B), values.rearrange("(b t) p h v -> b t p h v", b=B),
                   lambdas, neg_dram, y_all)
        output_stage(nc, x1, t["L0_attn_c_w"], y_all, x2, xn2)


def build(nc, t, out):
    x1 = nc.dram_tensor("x1", (B, NQ, D), F32, kind="Internal").ap()
    x2 = nc.dram_tensor("x2", (NTOK, D), F32, kind="Internal").ap()
    xn2 = nc.dram_tensor("xn2", (NTOK, D), F32, kind="Internal").ap()
    cross_attention(nc, t, x1)
    self_attention(nc, t, x1, x2, xn2)
    moe_stage(nc, x2, xn2, t["L0_ffn_combine_weights"], t["L0_ffn_top_idx"], t["L0_ffn_W1"], t["L0_ffn_b1"],
              t["L0_ffn_W2"], t["L0_ffn_b2"], out.rearrange("b q d -> (b q) d"))
```

```python
import math
from contextlib import ExitStack

import concourse.bass as bass
from concourse import mybir

F32 = mybir.dt.float32
F32R = mybir.dt.float32r
BF16 = mybir.dt.bfloat16
I32 = mybir.dt.int32
ALU = mybir.AluOpType
ACT = mybir.ActivationFunctionType
AX = mybir.AxisListType

P = 128
D = 256
DC = D // P
H = 16
DH = D // H
LN_EPS = 1e-5

B = 4
NQ = 256
NK = 4096
NTOK = B * NQ


ROWS = 52


def query_stage(nc, x, Wq, bq, mask, q_stacks, mask_rows):
    NT = NTOK // P
    NPAIR = H // 2
    with ExitStack() as ctx:
        def sb(name, shape, dt):
            return ctx.enter_context(nc.sbuf_tensor(name, shape, dt))

        def sem(name):
            return ctx.enter_context(nc.semaphore(name))

        x_in = sb("x_in", [P, NT, D], F32)
        xn = sb("xn", [P, NT, D], F32)
        xnT = sb("xnT", [P, DC, NTOK], F32)
        stats = sb("stats", [P, NT, 6], F32)
        mv = sb("mv", [P, NT, 2], F32)
        rstd = sb("rstd", [P, NT], F32)
        var_eps = sb("var_eps", [P, NT], F32)
        std = sb("std", [P, NT], F32)
        wq = sb("wq", [P, DC, D], F32)
        wq_rep = sb("wq_rep", [P, DC, H, 64], F32)
        bq_rep = sb("bq_rep", [P, NPAIR], F32)
        bq_scaled = sb("bq_scaled", [P, NPAIR], F32)
        lo_rows = sb("lo_rows", [P, 1], F32)
        consts = sb("consts", [P, NPAIR], F32)
        minus1 = sb("minus1", [P, 1], F32)
        ident = sb("ident_q", [P, P], F32)
        mask_i = sb("mask_i", [P, P], I32)
        mask_f = sb("mask_f", [P, P], F32)
        mask_hi = sb("mask_hi", [P, P], F32R)
        mask_lo = sb("mask_lo", [P, P], F32R)
        q_full = [sb(f"q_full{i}", [P, 512], F32) for i in range(2)]
        q_hi = [sb(f"q_hi{i}", [P, 512], F32R) for i in range(2)]
        q_out = [sb(f"q_out{i}", [P, 512], F32R) for i in range(2)]
        pt = [ctx.enter_context(nc.psum_tensor(f"pt{i}", [P, 512], F32)) for i in range(2)]
        pq = [ctx.enter_context(nc.psum_tensor(f"pq{i}", [P, 512], F32)) for i in range(2)]

        x_loaded = sem("x_loaded")
        w_loaded = sem("w_loaded")
        b_loaded = sem("b_loaded")
        mask_loaded = sem("mask_loaded")
        consts_set = sem("consts_set")
        ident_set = sem("ident_set")
        stats_done = sem("stats_done")
        std_done = sem("std_done")
        norm_done = sem("norm_done")
        rep_done = sem("rep_done")
        bias_done = sem("bias_done")
        mask_done = sem("mask_done")
        turned = sem("turned")
        turned_read = sem("turned_read")
        q_ready = sem("q_ready")
        full_done = sem("full_done")
        hi_done = sem("hi_done")
        out_done = sem("out_done")
        stored = [sem(f"stored{i}") for i in range(2)]
        mask_stored = sem("mask_stored")
        block = ctx.enter_context(nc.Block())

        @block.sync
        def _(sp):
            sp.dma_start(x_in[:], x.rearrange("b (t p) d -> p (b t) d", p=P)).then_inc(x_loaded, 16)
            sp.dma_start(wq[:], Wq.rearrange("(c p) n -> p c n", p=P)).then_inc(w_loaded, 16)
            sp.dma_start(mask_i[:], mask.rearrange("b u v (t f) -> (b u v t) f", f=P)).then_inc(mask_loaded, 16)
            sp.wait_ge(consts_set, 4)
            for j in range(2):
                for r in range(3):
                    row = 64 * j + 16 * r
                    sp.dma_start(bq_rep[row:row + DH, :], bq.rearrange("(n j d) -> j d n", j=2, d=DH)[j],
                                 allow_slow_non_contiguous=True).then_inc(b_loaded, 16)
                sp.dma_start(bq_rep[64 * j + 50:64 * j + 52, :], consts[0:2, :]).then_inc(b_loaded, 16)
                sp.dma_start(lo_rows[64 * j + 32:64 * j + 48, :], minus1[0:16, :]).then_inc(b_loaded, 16)
            sp.wait_ge(mask_done, 3)
            sp.dma_start(mask_rows[0].rearrange("b (t f) -> (b t) f", f=P), mask_hi[:].bitcast(F32)).then_inc(mask_stored, 16)
            sp.dma_start(mask_rows[1].rearrange("b (t f) -> (b t) f", f=P), mask_lo[:].bitcast(F32)).then_inc(mask_stored, 16)
            for n in range(2 * NPAIR):
                pair, half = n // 2, n % 2
                sp.wait_ge(out_done, n + 1)
                sp.dma_start(q_stacks[2 * half:2 * half + 2, pair // 2, :, pair % 2, :].rearrange("b p q -> p b q"),
                             q_out[n % 2][:].bitcast(F32).rearrange("p (b q) -> p b q", b=2)).then_inc(stored[n % 2], 16)
            sp.wait_ge(mask_stored, 32)
            for i in range(2):
                sp.wait_ge(stored[i], 16 * NPAIR)

        @block.gpsimd
        def _(pool):
            pool.memset(consts[:], 4.0).then_inc(consts_set, 1)
            pool.memset(minus1[:], -1.0).then_inc(consts_set, 1)
            pool.memset(bq_rep[:], 0.0).then_inc(consts_set, 1)
            pool.memset(lo_rows[:], 0.0).then_inc(consts_set, 1)
            pool.memset(ident[:], 0.0).then_inc(ident_set, 1)
            pool.wait_ge(ident_set, 1)
            pool.affine_select(out=ident[:], in_=ident[:], compare_op=ALU.not_equal, fill=1.0, base=0,
                               pattern=[[-1, P]], channel_multiplier=1).then_inc(ident_set, 1)
            pool.memset(wq_rep[:], 0.0).then_inc(rep_done, 1)
            pool.wait_ge(w_loaded, 16)
            pool.wait_ge(rep_done, 1)
            for c in range(DC):
                for r in range(3):
                    pool.tensor_copy(wq_rep[:, c, :, 16 * r:16 * r + DH],
                                     wq[:, c, :].rearrange("p (h d) -> p h d", d=DH)).then_inc(rep_done, 1)

        @block.vector
        def _(dve):
            dve.wait_ge(mask_loaded, 16)
            dve.tensor_scalar(mask_f[:], mask_i[:], -1e9, None, ALU.mult).then_inc(mask_done, 1)
            dve.wait_ge(mask_done, 1)
            dve.tensor_copy(mask_hi[:], mask_f[:]).then_inc(mask_done, 1)
            dve.wait_ge(mask_done, 2)
            dve.tensor_sub(mask_lo[:], mask_f[:], mask_hi[:].bitcast(F32)).then_inc(mask_done, 1)
            dve.wait_ge(x_loaded, 16)
            for t in range(NT):
                dve.bn_stats(stats[:, t, :], x_in[:, t, :]).then_inc(stats_done, 1)
            for t in range(NT):
                dve.wait_ge(stats_done, t + 1)
                dve.bn_aggr(mv[:, t, :], stats[:, t, :]).then_inc(stats_done, 1)
            dve.wait_ge(stats_done, 2 * NT)
            dve.tensor_scalar(var_eps[:], mv[:, :, 1], LN_EPS, None, ALU.add).then_inc(stats_done, 1)
            dve.wait_ge(std_done, 1)
            dve.reciprocal(rstd[:], std[:]).then_inc(stats_done, 1)
            dve.wait_ge(stats_done, 2 * NT + 2)
            for t in range(NT):
                dve.tensor_scalar(xn[:, t, :], x_in[:, t, :], mv[:, t, 0:1], rstd[:, t:t + 1],
                                  ALU.subtract, ALU.mult).then_inc(norm_done, 1)
            dve.wait_ge(b_loaded, 160)
            dve.tensor_scalar(bq_scaled[:], bq_rep[:], DH ** -0.5, None, ALU.mult).then_inc(bias_done, 1)
            for n in range(NT // 2 * DC):
                c, t4 = n % DC, n // DC
                if t4 * 4 >= NT:
                    break
                dve.wait_ge(turned, n + 1)
                dve.tensor_copy(xnT[:, c, t4 * 512:t4 * 512 + 512], pt[n % 2][:]).then_inc(turned_read, 1)
            for n in range(2 * NPAIR):
                dve.wait_ge(hi_done, n + 1)
                if n >= 2:
                    dve.wait_ge(stored[n % 2], 16 * (n // 2))
                dve.scalar_tensor_tensor(q_out[n % 2][:], q_hi[n % 2][:].bitcast(F32), lo_rows[:, 0:1],
                                         q_full[n % 2][:], ALU.mult, ALU.add).then_inc(out_done, 1)

        @block.tensor
        def _(pe):
            pe.wait_ge(ident_set, 2)
            for n in range(NT // 4 * DC):
                c, t4 = n % DC, n // DC
                pe.wait_ge(norm_done, 4 * t4 + 4)
                if n >= 2:
                    pe.wait_ge(turned_read, n - 1)
                for t in range(4):
                    mm = pe.transpose(pt[n % 2][:, t * P:(t + 1) * P], xn[:, 4 * t4 + t, c * P:(c + 1) * P], ident[:])
                mm.then_inc(turned, 1)
            pe.wait_ge(turned_read, NT // 4 * DC)
            pe.wait_ge(rep_done, 7)
            for n in range(2 * NPAIR):
                pair, half = n // 2, n % 2
                if n >= 2:
                    pe.wait_ge(full_done, n - 1)
                for c in range(DC):
                    mm = pe.matmul(pq[n % 2][:], wq_rep[:, c, 2 * pair:2 * pair + 2, :].rearrange("p h r -> p (h r)"),
                                   xnT[:, c, half * 512:half * 512 + 512], start=(c == 0), stop=(c == DC - 1))
                mm.then_inc(q_ready, 1)

        @block.scalar
        def _(act):
            act.wait_ge(stats_done, 2 * NT + 1)
            act.activation(std[:], var_eps[:], ACT.Sqrt).then_inc(std_done, 1)
            act.wait_ge(bias_done, 1)
            for n in range(2 * NPAIR):
                pair = n // 2
                act.wait_ge(q_ready, n + 1)
                if n >= 2:
                    act.wait_ge(out_done, n - 1)
                act.activation(q_full[n % 2][:], pq[n % 2][:], ACT.Identity, bias=bq_scaled[:, pair:pair + 1],
                               scale=DH ** -0.5).then_inc(full_done, 1)
                act.wait_ge(full_done, n + 1)
                act.activation(q_hi[n % 2][:], q_full[n % 2][:], ACT.Copy).then_inc(hi_done, 1)


QU = 4
KT = NK // P
STEPS = QU * KT
TAIL = STEPS
NMAX = 64
MAX_STEPS = 24


def misc_plan(last):
    jobs = []
    for q in range(QU):
        s0 = q * KT
        if q > 0:
            jobs.append((s0 + 3, "X", q - 1, 0))
        if q == 0:
            jobs += [(s0 + 5 + 2 * i, "K", 2, i) for i in range(8)]
        elif last:
            pass
        elif q == 1:
            jobs += [(s0 + (t if t < 3 else t + 1), "T", QU, t) for t in range(16)]
        elif q == 2:
            jobs += [(s0 + 5 + 2 * i, "K", QU, i) for i in range(8)]
        else:
            jobs += [(s0 + 4 + 2 * j, "V", QU, j) for j in range(16)]
        if not (last and q == 3):
            jobs.append((s0 + MAX_STEPS + 1, "M", q + 1, 0))
    jobs += [(TAIL, "X", 3, 0), (TAIL, "W", 0, 0)]
    jobs = [(min(s, TAIL), *rest) for s, *rest in jobs]
    order = sorted(range(len(jobs)), key=lambda n: (jobs[n][0], jobs[n][1] != "X", n))
    return [jobs[n] for n in order]


FIRST_JOBS = [("T", 0, 0), ("T", 0, 1)]
FIRST_JOBS += [j for i in range(7) for j in (("T", 0, 2 * i + 2), ("T", 0, 2 * i + 3), ("K", 0, i))] + [("K", 0, 7)]
FIRST_JOBS += [("V", 0, j) for j in range(16)] + [("M", 0, 0)]

JOB_COST = {"T": 0.6, "K": 0.7, "V": 1.8, "M": 0.2, "X": 0.5, "W": 0.0}


def max_jobs_at(q, kt):
    cost = [1.4] * MAX_STEPS
    for step, kind, _, _ in misc_plan(False):
        if step // KT == q and step % KT < MAX_STEPS:
            cost[step % KT] += JOB_COST[kind]
    bounds = [round(NMAX * sum(cost[:n]) / sum(cost)) for n in range(MAX_STEPS + 1)]
    return range(bounds[kt], bounds[kt + 1]) if kt < MAX_STEPS else range(0)


def max_job(n):
    return n // 8, (n // 4) % 2, (n // 2) % 2, n % 2


def cross_stage(nc, x, ctx_in, Wk, bk, Wv, bv, Wo, bo, q_stacks, mask_rows, x1):
    NJ = len(misc_plan(False))
    NF = len(FIRST_JOBS)
    with ExitStack() as ctx:
        def sb(name, shape, dt):
            return ctx.enter_context(nc.sbuf_tensor(name, shape, dt))

        def sem(name):
            return ctx.enter_context(nc.semaphore(name))

        def psum(name, shape):
            return ctx.enter_context(nc.psum_tensor(name, shape, F32))

        stack = [sb(f"stack{i}", [P, 2, NK], F32R) for i in range(2)]
        k_hi = sb("k_hi", [P, NK], F32R)
        k_lo = sb("k_lo", [P, NK], F32R)
        ctxT = sb("ctxT", [P, DC, NK], F32)
        raw = [sb(f"raw{i}", [P, 2, D], F32) for i in range(2)]
        val = sb("val", [P, KT, H, DH + 1], F32)
        qs = sb("qs", [P, QU, 2, NQ], F32R)
        prob = [sb(f"prob{i}", [P, 2, 2, NQ], F32) for i in range(2)]
        wk = sb("wk", [P, DC, D], F32)
        wv = sb("wv", [P, DC, D], F32)
        wo = sb("wo", [P, QU, D], F32)
        bk_u = sb("bk_u", [P, 2], F32)
        bv_u = sb("bv_u", [P, QU], F32)
        bo_r = sb("bo_r", [1, D], F32)
        ones_r = sb("ones_r", [1, P], F32)
        ident = sb("ident", [P, P], F32)
        den_sel = sb("den_sel", [P, P], F32)
        max_parts = sb("max_parts", [P, 8, 8], F32)
        neg_max = sb("neg_max", [P, 8], F32)
        neg_hi = sb("neg_hi", [P, 8], F32R)
        neg_cols = sb("neg_cols", [P, 4, 2, 2], F32)
        neg_rows = sb("neg_rows", [16, P], F32R)
        head_out = sb("head_out", [P, NQ], F32)
        rden = sb("rden", [P, NQ], F32)
        normed = sb("normed", [P, NQ], F32)
        heads = sb("heads", [P, QU, NQ], F32)
        x_res = sb("x_res", [P, 2, D], F32)
        x_out = sb("x_out", [P, 2, D], F32)
        score = [psum(f"score{i}", [P, 2, 2, NQ]) for i in range(2)]
        mx = [psum(f"mx{i}", [P, 512]) for i in range(2)]
        misc = psum("misc", [P, 512])
        acc = psum("acc", [P, 512])

        w_loaded = sem("w_loaded_x")
        zeroed = sem("zeroed")
        ident_set = sem("ident_set_x")
        ones_set = sem("ones_set_x")
        consts_set = sem("consts_set_x")
        raw_loaded = [sem(f"raw_loaded{i}") for i in range(2)]
        q_loaded = [sem(f"q_loaded{i}") for i in range(QU)]
        k_stacked = [[sem(f"k_stacked{i}{h}") for h in range(2)] for i in range(2)]
        mask_stacked = [[sem(f"mask_stacked{i}{h}") for h in range(2)] for i in range(2)]
        neg_stacked = sem("neg_stacked")
        res_loaded = sem("res_loaded")
        x1_stored = sem("x1_stored")
        scored = sem("scored")
        exp_done = sem("exp_done")
        pv_done = sem("pv_done")
        max_ready = sem("max_ready")
        max_read = sem("max_read")
        misc_ready = sem("misc_ready")
        misc_read = sem("misc_read")
        first_act = sem("first_act")
        first_dve = sem("first_dve")
        khi_done = sem("khi_done")
        passed = sem("passed")
        neg_found = sem("neg_found")
        neg_split = sem("neg_split")
        neg_turnable = sem("neg_turnable")
        acc_read = sem("acc_read")
        normed_done = sem("normed_done")
        heads_done = sem("heads_done")
        block = ctx.enter_context(nc.Block())

        def index_of(jobs_list, kind, unit, i):
            return [j[-3:] for j in jobs_list].index((kind, unit, i))

        def job_count(b, last, kind, unit, i):
            return NF + b * NJ + index_of(misc_plan(last), kind, unit, i) + 1

        def first_count(kind, unit, i):
            return index_of(FIRST_JOBS, kind, unit, i) + 1

        first_banks = [misc[:]] + [score[n // 2][:, n % 2, :, :].rearrange("p a q -> p (a q)") for n in range(3)]

        def first_bank(n):
            return first_banks[n % 4] if FIRST_JOBS[n][0] != "M" else misc[:]

        def first_reader(n):
            acts = FIRST_JOBS[n][0] in "TV"
            return (first_act if acts else first_dve), sum((j[0] in "TV") == acts for j in FIRST_JOBS[:n + 1])

        def wait_apart(eng, sem, count):
            eng.wait_ge(sem, count)
            eng.sem_inc(passed, 1)

        def all_batches(eng, body):
            with eng.Fori(0, B - 1) as b:
                body(b, False)
            body(B - 1, True)

        @block.gpsimd
        def _(pool):
            def load_ctx(b, t, free):
                if free is not None:
                    pool.wait_ge(misc_ready, free)
                pool.dma_start(raw[t % 2][:], ctx_in[b, 2 * P * t:2 * P * (t + 1), :]
                               .rearrange("(i p) d -> p i d", p=P)).then_inc(raw_loaded[t % 2], 16)

            def load_q(b, q):
                pool.dma_start(qs[:, q, :, :].bitcast(F32), q_stacks[b, q]).then_inc(q_loaded[q], 16)

            def load_mask(b, i, h, which=range(4)):
                for j, pair in ((0, 0), (0, 1), (1, 0), (1, 1)):
                    if 2 * j + pair in which:
                        pool.dma_start(stack[i][64 * j + 50:64 * j + 52, pair, h * 2048:(h + 1) * 2048].bitcast(F32),
                                       mask_rows[:, b, h * 2048:(h + 1) * 2048]).then_inc(mask_stacked[i][h], 16)

            load_ctx(0, 0, None)
            load_ctx(0, 1, None)
            pool.memset(ident[:], 0.0).then_inc(ident_set, 1)
            pool.wait_ge(ident_set, 1)
            pool.affine_select(out=ident[:], in_=ident[:], compare_op=ALU.not_equal, fill=1.0, base=0,
                               pattern=[[-1, P]], channel_multiplier=1).then_inc(ident_set, 1)
            pool.memset(wo[:], 0.0).then_inc(zeroed, 1)
            pool.memset(bv_u[:], 0.0).then_inc(zeroed, 1)
            for t in range(2, 16):
                load_ctx(0, t, first_count("T", 0, t - 2))
                if 4 <= t < 8:
                    load_q(0, t - 4)
                elif t >= 8:
                    load_mask(0, (t - 8) // 4, (t - 8) // 2 % 2, ((0, 1), (2, 3))[t % 2])
                if t == 7:
                    pool.wait_ge(ones_set, 3)
                if t == 3:
                    pool.memset(den_sel[:], 0.0).then_inc(zeroed, 1)
                    pool.memset(head_out[:], 0.0).then_inc(zeroed, 1)
                    pool.memset(ones_r[:], 1.0).then_inc(zeroed, 1)
                    v = den_sel[:].rearrange("p (h r) -> p h r", h=4)
                    pool.wait_ge(zeroed, 5)
                    pool.affine_select(out=v, in_=v, compare_op=ALU.not_equal, fill=1.0, base=-DH,
                                       pattern=[[-32, 4], [0, 32]], channel_multiplier=1).then_inc(consts_set, 1)
            pool.dma_start(x_res[:], x[0].rearrange("(i p) d -> p i d", p=P)).then_inc(res_loaded, 16)

            def body(b, last):
                if last:
                    return
                load_ctx(b + 1, 0, NF + b * NJ)
                load_ctx(b + 1, 1, NF + b * NJ)
                pool.wait_ge(scored, STEPS * b + KT)
                load_q(b + 1, 0)
                for t in range(2, 16):
                    load_ctx(b + 1, t, job_count(b, False, "T", QU, t - 2))
                pool.wait_ge(scored, STEPS * b + 2 * KT)
                load_q(b + 1, 1)
                for i in range(2):
                    wait_apart(pool, scored, STEPS * b + KT * (i + 2) + KT // 2)
                    load_mask(b + 1, i, 0)
                    wait_apart(pool, scored, STEPS * b + KT * (i + 3))
                    load_mask(b + 1, i, 1)
                    load_q(b + 1, i + 2)
                pool.wait_ge(misc_read, job_count(b, False, "W", 0, 0))
                pool.dma_start(x_res[:], x[b + 1].rearrange("(i p) d -> p i d", p=P)).then_inc(res_loaded, 16)

            all_batches(pool, body)

        @block.sync
        def _(sp):
            sp.sem_inc(x1_stored, 16)
            sp.dma_start(wk[:], Wk.rearrange("(c p) n -> p c n", p=P)).then_inc(w_loaded, 16)
            sp.dma_start(wv[:], Wv.rearrange("(c p) n -> p c n", p=P)).then_inc(w_loaded, 16)
            sp.dma_start(bo_r[:], bo.rearrange("(a n) -> a n", a=1)).then_inc(w_loaded, 16)
            sp.dma_start(bk_u[:], bk.rearrange("(g p) -> p g", g=2), allow_slow_non_contiguous=True)\
                .then_inc(w_loaded, 16)
            sp.wait_ge(zeroed, 2)
            for hq in range(4):
                sp.dma_start(wo[32 * hq:32 * hq + DH, :, :], Wo.rearrange("(q h d) n -> h d q n", q=QU, h=4)[hq])\
                    .then_inc(w_loaded, 16)
                sp.dma_start(bv_u[32 * hq:32 * hq + DH, :], bv.rearrange("(q h d) -> h d q", q=QU, h=4)[hq],
                             allow_slow_non_contiguous=True).then_inc(w_loaded, 16)

            def stack_keys(q, h):
                for hq in range(4):
                    pair, j = hq // 2, hq % 2
                    i = q % 2
                    src = slice(64 * i + 16 * hq, 64 * i + 16 * hq + DH)
                    for r, part in enumerate((k_hi, k_lo, k_hi)):
                        sp.dma_start(stack[i][64 * j + 16 * r:64 * j + 16 * r + DH, pair, h * 2048:(h + 1) * 2048]
                                     .bitcast(F32), part[src, h * 2048:(h + 1) * 2048].bitcast(F32)).then_inc(k_stacked[i][h], 16)

            def stack_max(q):
                for hq in range(4):
                    pair, j = hq // 2, hq % 2
                    for qh in range(2):
                        row = 4 * hq + 2 * qh
                        sp.dma_start(qs[64 * j + 48:64 * j + 50, q, pair, qh * P:(qh + 1) * P].bitcast(F32),
                                     neg_rows[row:row + 2, :].bitcast(F32)).then_inc(neg_stacked, 16)

            sp.wait_ge(ones_set, 3)
            for h in range(2):
                sp.wait_ge(*first_reader(index_of(FIRST_JOBS, "K", 0, 4 * h + 3)))
                stack_keys(0, h)
            for h in range(2):
                stack_keys(1, h)
            sp.wait_ge(*first_reader(NF - 1))
            stack_max(0)

            def body(b, last):
                for q in range(QU):
                    if not (last and q >= 2):
                        if q % 2 == 0:
                            wait_apart(sp, misc_read, job_count(b, last, "K", q + 2, 7))
                        sp.wait_ge(scored, STEPS * b + KT * q + KT // 2)
                        stack_keys(q, 0)
                    if not (last and q == 3):
                        sp.wait_ge(misc_read, job_count(b, last, "M", q + 1, 0))
                        stack_max((q + 1) % QU)
                    if not (last and q >= 2):
                        sp.wait_ge(scored, STEPS * b + KT * (q + 1))
                        stack_keys(q, 1)
                sp.wait_ge(misc_read, job_count(b, last, "W", 0, 0))
                sp.dma_start(x1[b].rearrange("(i p) d -> p i d", p=P), x_out[:]).then_inc(x1_stored, 16)

            all_batches(sp, body)
            sp.wait_ge(x1_stored, 16 * (B + 1))

        @block.tensor
        def _(pe):
            pe.wait_ge(ident_set, 2)

            def job(count, kind, b, u, i, t_count, misc=misc):
                if count is not None:
                    pe.wait_ge(misc_read, count)
                if kind == "T":
                    pe.wait_ge(raw_loaded[i % 2], 16 * (8 * b + i // 2 + 1))
                    for t in range(2):
                        for c in range(DC):
                            mm = pe.transpose(misc[:, c * 256 + t * P:c * 256 + (t + 1) * P],
                                              raw[i % 2][:, t, c * P:(c + 1) * P], ident[:])
                elif kind == "K":
                    g = u % QU // 2
                    for c in range(DC):
                        mm = pe.matmul(misc[:], wk[:, c, P * g:P * (g + 1)], ctxT[:, c, i * 512:(i + 1) * 512],
                                       start=(c == 0), stop=(c == DC - 1))
                elif kind == "V":
                    for t in range(2):
                        for c in range(DC):
                            mm = pe.matmul(misc[:, t * 256:(t + 1) * 256], ctxT[:, c, (2 * i + t) * P:(2 * i + t + 1) * P],
                                           wv[:, c, :], start=(c == 0), stop=(c == DC - 1))
                elif kind == "M":
                    pe.wait_ge(neg_turnable, t_count)
                    mm = pe.transpose(misc[0:16, 0:P], neg_cols[:].rearrange("p a b c -> p (a b c)"), ident[:])
                elif kind == "X":
                    pe.wait_ge(acc_read, t_count)
                    mm = pe.matmul(misc[:, 0:NQ], den_sel[:], head_out[:], start=True, stop=True)
                elif kind == "W":
                    pe.wait_ge(heads_done, t_count)
                    for t in range(2):
                        out = misc[:, t * 256:(t + 1) * 256]
                        pe.matmul(out, ones_r[:], bo_r[:], start=True, stop=False)
                        for q in range(QU):
                            mm = pe.matmul(out, heads[:, q, t * P:(t + 1) * P], wo[:, q, :],
                                           start=False, stop=(q == QU - 1))
                mm.then_inc(misc_ready, 1)

            def max_tile(n, i, q, use, batch, count):
                chunk, pair, qh, j = max_job(n)
                if n % 32 == 0:
                    h = n // 32
                    pe.wait_ge(k_stacked[i][h], 16 * 12 * (use + 1))
                    if q < 2:
                        pe.wait_ge(mask_stacked[i][h], 64 * (batch + 1))
                if count is not None:
                    pe.wait_ge(max_read, count)
                pe.matmul(mx[j][:], qs[64 * j:64 * j + ROWS, q, pair, qh * P:(qh + 1) * P],
                          stack[i][64 * j:64 * j + ROWS, pair, chunk * 512:(chunk + 1) * 512],
                          start=True, stop=True).then_inc(max_ready, 1)

            def pv(b, s):
                q, kt = s // KT, s % KT
                pe.wait_ge(exp_done, STEPS * b + s + 1)
                if kt == 0 and q > 0:
                    pe.wait_ge(acc_read, 4 * b + q)
                for hq in range(4):
                    mm = pe.matmul(acc[32 * hq:32 * hq + DH + 1, 0:NQ], val[:, kt, 4 * q + hq, :],
                                   prob[s % 2][:, hq % 2, hq // 2, :], start=(kt == 0), stop=(kt == KT - 1))
                mm.then_inc(pv_done, 1)

            def scores(b, s):
                q, kt = s // KT, s % KT
                if kt == 0:
                    pe.wait_ge(neg_stacked, 16 * 8 * (4 * b + q + 1))
                if not (isinstance(b, int) and b == 0 and s < 2):
                    pe.wait_ge(exp_done, STEPS * b + s - 1)
                for hq in range(4):
                    pair, j = hq // 2, hq % 2
                    mm = pe.matmul(score[s % 2][:, j, pair, :],
                                   stack[q % 2][64 * j:64 * j + ROWS, pair, kt * P:(kt + 1) * P],
                                   qs[64 * j:64 * j + ROWS, q, pair, :], start=True, stop=True)
                mm.then_inc(scored, 1)

            for n, (kind, u, i) in enumerate(FIRST_JOBS):
                if kind == "K" and i == 0:
                    pe.wait_ge(w_loaded, 16 * 12)
                if kind == "V":
                    if i == 0:
                        pe.wait_ge(consts_set, 1)
                        pe.wait_ge(ones_set, 3)
                        pe.wait_ge(q_loaded[0], 16)
                    for m in range(4 * i, 4 * i + 4):
                        max_tile(m, 0, 0, 0, 0, m - 1 if m >= 2 else None)
                if kind == "M":
                    pe.wait_ge(*first_reader(max(m for m in range(n) if m % 4 == 0)))
                elif n >= 4:
                    pe.wait_ge(*first_reader(n - 4))
                if kind == "K":
                    pe.wait_ge(*first_reader(index_of(FIRST_JOBS, "T", 0, 2 * i + 1)))
                job(None, kind, 0, u, i, 2, first_bank(n))
            pe.wait_ge(misc_read, NF)
            for s in range(2):
                scores(0, s)

            def body(b, last):
                plan = misc_plan(last)
                count = 0
                pe.wait_ge(misc_read, NF + b * NJ)
                for s in range(STEPS + 1):
                    q, kt = s // KT, s % KT
                    if s < STEPS:
                        tiles = [] if last and q == 3 else list(max_jobs_at(q, kt))
                        nb, qn = b + (q + 1) // QU, (q + 1) % QU
                        if kt == 0 and tiles:
                            pe.wait_ge(q_loaded[qn], 16 * (nb + 1))

                        slots = {2: (0, 2), 1: (1,)}.get(len(tiles), range(4))

                        def max_slot(i):
                            for n in (tiles[:] if i == 3 else tiles[:1] if i in slots else []):
                                tiles.remove(n)
                                max_tile(n, qn % 2, qn, 2 * b + (q + 1) // 2, nb, NMAX * (4 * b + q + 1) + n - 1)

                        max_slot(0)
                        if s >= 2:
                            scores(b, s)
                        max_slot(1)
                    if s == TAIL:
                        if not last:
                            scores(b + 1, 0)
                        pv(b, s - 1)
                        if not last:
                            scores(b + 1, 1)
                    while count < len(plan) and plan[count][0] == s:
                        _, kind, u, i = plan[count]
                        need = {"M": 2 * (4 * b + u + 1), "X": 4 * b + u + 1, "W": 4 * b + 4}.get(kind)
                        job(NF + b * NJ + count, kind, b + u // QU, u, i, need)
                        count += 1
                    if s == TAIL:
                        break
                    max_slot(2)
                    if s >= 1:
                        pv(b, s - 1)
                    max_slot(3)

            all_batches(pe, body)

        @block.scalar
        def _(act):
            act.wait_ge(w_loaded, 16 * 12)

            def evacuate(count, kind, u, i, staged, pv_count, misc=misc, misc_read=misc_read):
                act.wait_ge(misc_ready, count + 1)
                if kind == "T":
                    act.activation(ctxT[:, :, i * 256:(i + 1) * 256], misc[:].rearrange("p (c n) -> p c n", c=DC),
                                   ACT.Copy).then_inc(misc_read, 1)
                elif kind == "K":
                    if i == 0 and staged is not None:
                        for h in range(2):
                            act.wait_ge(k_stacked[0][h], 16 * 12 * staged)
                            act.wait_ge(k_stacked[1][h], 16 * 12 * staged)
                    g = u % QU // 2
                    act.activation(k_hi[:, i * 512:(i + 1) * 512], misc[:], ACT.Identity, bias=bk_u[:, g:g + 1]).then_inc(khi_done, 1)
                elif kind == "V":
                    if pv_count is not None:
                        act.wait_ge(pv_done, pv_count)
                    act.activation(val[:, 2 * i:2 * i + 2, :, 0:DH],
                                   misc[:].rearrange("p (t h d) -> p t h d", t=2, h=H), ACT.Copy).then_inc(misc_read, 1)

            act.wait_ge(ones_set, 1)
            for n, (kind, u, i) in enumerate(FIRST_JOBS):
                if kind in "TKV":
                    evacuate(n, kind, u, i, None, None, first_bank(n), first_act)
            act.wait_ge(*first_reader(NF - 1))
            act.wait_ge(*first_reader(NF - 2))
            act.sem_inc(misc_read, NF)

            def body(b, last):
                plan = misc_plan(last)
                count = 0
                for s in range(STEPS + 1):
                    if s < STEPS:
                        act.wait_ge(scored, STEPS * b + s + 1)
                        if s >= 2:
                            act.wait_ge(pv_done, STEPS * b + s - 1)
                        act.activation(prob[s % 2][:], score[s % 2][:], ACT.Exp).then_inc(exp_done, 1)
                    while count < len(plan) and plan[count][0] == s:
                        _, kind, u, i = plan[count]
                        if kind in "TKV":
                            evacuate(NF + b * NJ + count, kind, u, i, 2 * b + u // 2,
                                     STEPS * b + 3 * KT + 2 * i + 2)
                        count += 1

            all_batches(act, body)

        @block.vector
        def _(dve):
            dve.memset(val[:, :, :, DH:DH + 1], 1.0).then_inc(ones_set, 1)
            for i in range(2):
                dve.memset(stack[i][:].bitcast(F32), 1.0).then_inc(ones_set, 1)
            dve.wait_ge(w_loaded, 16 * 12)
            dve.wait_ge(consts_set, 1)

            def max_read_tile(n, unit):
                chunk, pair, qh, j = max_job(n)
                dve.wait_ge(max_ready, NMAX * unit + n + 1)
                dve.tensor_reduce(max_parts[:, (2 * pair + j) * 2 + qh, chunk:chunk + 1], mx[j][:], AX.X, ALU.max)\
                    .then_inc(max_read, 1)

            def columns(unit):
                dve.wait_ge(max_read, NMAX * unit + NMAX)
                dve.tensor_reduce(neg_max[:], max_parts[:], AX.X, ALU.max, negate=True).then_inc(neg_found, 1)
                dve.wait_ge(neg_found, unit + 1)
                dve.tensor_copy(neg_hi[:], neg_max[:]).then_inc(neg_split, 1)
                dve.wait_ge(neg_split, unit + 1)
                hi = neg_hi[:].bitcast(F32).rearrange("p (h a) -> p h a", a=2)
                dve.tensor_copy(neg_cols[:, :, :, 0], hi).then_inc(neg_turnable, 1)
                dve.tensor_sub(neg_cols[:, :, :, 1], neg_max[:].rearrange("p (h a) -> p h a", a=2), hi)\
                    .then_inc(neg_turnable, 1)

            def evacuate(b, count, kind, u, i, first=False, misc=misc, misc_read=misc_read):
                if kind == "K":
                    g = u % QU // 2
                    dve.wait_ge(khi_done, 8 * (2 * b + u // 2) + i + 1)
                    dve.scalar_tensor_tensor(k_lo[:, i * 512:(i + 1) * 512], misc[:], bk_u[:, g:g + 1],
                                             k_hi[:, i * 512:(i + 1) * 512].bitcast(F32), ALU.add, ALU.subtract)\
                        .then_inc(misc_read, 1)
                elif kind == "M":
                    dve.wait_ge(misc_ready, count + 1)
                    if not first:
                        dve.wait_ge(neg_stacked, 16 * 8 * (4 * b + u))
                    dve.tensor_copy(neg_rows[:], misc[0:16, 0:P]).then_inc(misc_read, 1)
                elif kind == "X":
                    dve.wait_ge(misc_ready, count + 1)
                    dve.reciprocal(rden[:], misc[:, 0:NQ]).then_inc(misc_read, 1)
                    dve.wait_ge(misc_read, count + 1)
                    dve.tensor_mul(normed[:], head_out[:], rden[:]).then_inc(normed_done, 1)
                    dve.wait_ge(normed_done, 4 * b + u + 1)
                    dve.tensor_scalar(heads[:, u, :], normed[:], bv_u[:, u:u + 1], None, ALU.add)\
                        .then_inc(heads_done, 1)
                elif kind == "W":
                    dve.wait_ge(misc_ready, count + 1)
                    dve.wait_ge(res_loaded, 16 * (b + 1))
                    dve.wait_ge(x1_stored, 16 * (b + 1))
                    dve.tensor_add(x_out[:].rearrange("p i d -> p (i d)"), misc[:],
                                   x_res[:].rearrange("p i d -> p (i d)")).then_inc(misc_read, 1)

            def read_acc(b, q):
                dve.wait_ge(pv_done, STEPS * b + KT * (q + 1))
                for hq in range(4):
                    cp = dve.tensor_copy(head_out[32 * hq:32 * hq + DH + 1, :], acc[32 * hq:32 * hq + DH + 1, 0:NQ])
                cp.then_inc(acc_read, 1)

            for n, (kind, u, i) in enumerate(FIRST_JOBS):
                if kind == "V":
                    for m in range(4 * i, 4 * i + 4):
                        max_read_tile(m, 0)
                if kind == "M":
                    columns(0)
                if kind in "KM":
                    evacuate(0, n, kind, u, i, first=True, misc=first_bank(n), misc_read=first_dve)

            def body(b, last):
                plan = misc_plan(last)
                count = 0
                for s in range(STEPS + 1):
                    q, kt = s // KT, s % KT
                    if kt == 1 and q > 0:
                        read_acc(b, q - 1)
                    if s == TAIL:
                        read_acc(b, QU - 1)
                    if s < STEPS and not (last and q == 3):
                        for n in max_jobs_at(q, kt):
                            max_read_tile(n, 4 * b + q + 1)
                        if kt == MAX_STEPS:
                            columns(4 * b + q + 1)
                    while count < len(plan) and plan[count][0] == s:
                        _, kind, u, i = plan[count]
                        if kind in "KMXW":
                            evacuate(b, NF + b * NJ + count, kind, u, i)
                        count += 1

            all_batches(dve, body)


MAX_ROWS = 48
EXP_ROWS = 50
VD = 2 * DH
VW = VD + 1
LAMBDA_INIT = 0.8 - 0.6 * math.exp(-0.3 * (4 - 1))
MASKED = -1e30


def project_stage(nc, x1, weights, v_w, parts, values):
    NT = NTOK // P
    NB = 4
    with ExitStack() as ctx:
        def sb(name, shape, dt):
            return ctx.enter_context(nc.sbuf_tensor("p_" + name, shape, dt))

        def sem(name):
            return ctx.enter_context(nc.semaphore("p_" + name))

        x_in = sb("x_in", [P, NT, D], F32)
        xn = sb("xn", [P, NT, D], F32)
        xnT = sb("xnT", [P, DC, NTOK], F32)
        stats = sb("stats", [P, NT, 6], F32)
        mv = sb("mv", [P, NT, 2], F32)
        var_eps = sb("var_eps", [P, NT], F32)
        std = sb("std", [P, NT], F32)
        rstd = sb("rstd", [P, NT], F32)
        w = [sb(f"w{i}", [P, DC, D], F32) for i in range(4)]
        wv = sb("wv", [P, DC, 2 * D], F32)
        ident = sb("ident", [P, P], F32)
        hi = [sb(f"hi{i}", [P, 512], F32R) for i in range(NB)]
        lo = [sb(f"lo{i}", [P, 512], F32R) for i in range(NB)]
        vals = [sb(f"vals{i}", [P, H, VW], F32) for i in range(2)]
        pt = [ctx.enter_context(nc.psum_tensor(f"p_pt{i}", [P, 512], F32)) for i in range(2)]
        pp = [ctx.enter_context(nc.psum_tensor(f"p_pp{i}", [P, 512], F32)) for i in range(NB)]

        x_loaded, w_loaded, ident_set, ones_set = sem("x_loaded"), sem("w_loaded"), sem("ident_set"), sem("ones_set")
        stats_done, std_done, norm_done = sem("stats_done"), sem("std_done"), sem("norm_done")
        turned, turned_read = sem("turned"), sem("turned_read")
        projected, hi_done, lo_done = sem("projected"), sem("hi_done"), sem("lo_done")
        stored = [sem(f"stored{i}") for i in range(NB)]
        v_done = sem("v_done")
        v_stored = [sem(f"v_stored{i}") for i in range(2)]
        NPJ = 16
        block = ctx.enter_context(nc.Block())

        @block.sync
        def _(sp):
            sp.dma_start(x_in[:], x1.rearrange("b (t p) d -> p (b t) d", p=P)).then_inc(x_loaded, 16)
            for i in range(4):
                sp.dma_start(w[i][:], weights[i].rearrange("(c p) n -> p c n", p=P)).then_inc(w_loaded, 16)
            sp.dma_start(wv[:], v_w.rearrange("(c p) n -> p c n", p=P)).then_inc(w_loaded, 16)
            for n in range(NPJ):
                i, g, half = n // 4, n // 2 % 2, n % 2
                sp.wait_ge(lo_done, n + 1)
                for part, tile in enumerate((hi, lo)):
                    sp.dma_start(parts[i, part, g * P:(g + 1) * P, half * 512:(half + 1) * 512],
                                 tile[n % NB][:].bitcast(F32)).then_inc(stored[n % NB], 16)
            for t in range(NT):
                sp.wait_ge(v_done, t + 1)
                sp.dma_start(values[t], vals[t % 2][:]).then_inc(v_stored[t % 2], 16)
            for i in range(NB):
                sp.wait_ge(stored[i], 32 * NPJ // NB)
            for i in range(2):
                sp.wait_ge(v_stored[i], 16 * NT // 2)

        @block.gpsimd
        def _(pool):
            pool.memset(ident[:], 0.0).then_inc(ident_set, 1)
            pool.wait_ge(ident_set, 1)
            pool.affine_select(out=ident[:], in_=ident[:], compare_op=ALU.not_equal, fill=1.0, base=0,
                               pattern=[[-1, P]], channel_multiplier=1).then_inc(ident_set, 1)
            for i in range(2):
                pool.memset(vals[i][:], 1.0).then_inc(ones_set, 1)

        @block.vector
        def _(dve):
            dve.wait_ge(x_loaded, 16)
            for t in range(NT):
                dve.bn_stats(stats[:, t, :], x_in[:, t, :]).then_inc(stats_done, 1)
            for t in range(NT):
                dve.wait_ge(stats_done, t + 1)
                dve.bn_aggr(mv[:, t, :], stats[:, t, :]).then_inc(stats_done, 1)
            dve.wait_ge(stats_done, 2 * NT)
            dve.tensor_scalar(var_eps[:], mv[:, :, 1], LN_EPS, None, ALU.add).then_inc(stats_done, 1)
            dve.wait_ge(std_done, 1)
            dve.reciprocal(rstd[:], std[:]).then_inc(stats_done, 1)
            dve.wait_ge(stats_done, 2 * NT + 2)
            for t in range(NT):
                dve.tensor_scalar(xn[:, t, :], x_in[:, t, :], mv[:, t, 0:1], rstd[:, t:t + 1],
                                  ALU.subtract, ALU.mult).then_inc(norm_done, 1)
            for n in range(NT // 4 * DC):
                c, t4 = n % DC, n // DC
                dve.wait_ge(turned, n + 1)
                dve.tensor_copy(xnT[:, c, t4 * 512:t4 * 512 + 512], pt[n % 2][:]).then_inc(turned_read, 1)
            for n in range(NPJ):
                dve.wait_ge(hi_done, n + 1)
                dve.scalar_tensor_tensor(lo[n % NB][:], pp[n % NB][:], DH ** -0.5 if n // 4 < 2 else 1.0,
                                         hi[n % NB][:].bitcast(F32), ALU.mult, ALU.subtract).then_inc(lo_done, 1)

        @block.tensor
        def _(pe):
            pe.wait_ge(ident_set, 2)
            for n in range(NT // 4 * DC):
                c, t4 = n % DC, n // DC
                pe.wait_ge(norm_done, 4 * t4 + 4)
                if n >= 2:
                    pe.wait_ge(turned_read, n - 1)
                for t in range(4):
                    mm = pe.transpose(pt[n % 2][:, t * P:(t + 1) * P], xn[:, 4 * t4 + t, c * P:(c + 1) * P], ident[:])
                mm.then_inc(turned, 1)
            pe.wait_ge(turned_read, NT // 4 * DC)
            pe.wait_ge(w_loaded, 80)
            for n in range(NPJ):
                i, g, half = n // 4, n // 2 % 2, n % 2
                if n >= NB:
                    pe.wait_ge(lo_done, n - NB + 1)
                for c in range(DC):
                    mm = pe.matmul(pp[n % NB][:], w[i][:, c, g * P:(g + 1) * P],
                                   xnT[:, c, half * 512:half * 512 + 512], start=(c == 0), stop=(c == DC - 1))
                mm.then_inc(projected, 1)
            for t in range(NT):
                pe.wait_ge(*((lo_done, NPJ - NB + 1 + t) if t < NB else (v_done, t - NB + 1)))
                for c in range(DC):
                    mm = pe.matmul(pp[t % NB][:], xnT[:, c, t * P:(t + 1) * P], wv[:, c, :],
                                   start=(c == 0), stop=(c == DC - 1))
                mm.then_inc(projected, 1)

        @block.scalar
        def _(act):
            act.wait_ge(stats_done, 2 * NT + 1)
            act.activation(std[:], var_eps[:], ACT.Sqrt).then_inc(std_done, 1)
            for n in range(NPJ):
                act.wait_ge(projected, n + 1)
                if n >= NB:
                    act.wait_ge(stored[n % NB], 32 * (n // NB))
                act.activation(hi[n % NB][:], pp[n % NB][:], ACT.Copy, scale=DH ** -0.5 if n // 4 < 2 else 1.0)\
                    .then_inc(hi_done, 1)
            act.wait_ge(ones_set, 2)
            for t in range(NT):
                act.wait_ge(projected, NPJ + t + 1)
                if t >= 2:
                    act.wait_ge(v_stored[t % 2], 16 * (t // 2))
                act.activation(vals[t % 2][:, :, 0:VD], pp[t % NB][:].rearrange("p (h d) -> p h d", h=H),
                               ACT.Copy).then_inc(v_done, 1)


def diff_stage(nc, parts, values, lambdas, neg_dram, y_all, var_eps):
    NPAIR = H // 2
    with ExitStack() as ctx:
        def sb(name, shape, dt):
            return ctx.enter_context(nc.sbuf_tensor("d_" + name, shape, dt))

        def sem(name):
            return ctx.enter_context(nc.semaphore("d_" + name))

        def psum(name, shape):
            return ctx.enter_context(nc.psum_tensor("d_" + name, shape, F32))

        stack = [[sb(f"stack{b}{i}", [P, NPAIR, NQ], F32R) for i in range(4)] for b in range(2)]
        val = [sb(f"val{b}", [P, 2, H, VW], F32) for b in range(2)]
        prob = [sb(f"prob{i}", [P, 2, 512], F32) for i in range(6)]
        head_sum = sb("head_sum", [P, 4], F32)
        neg_mean = sb("neg_mean", [P, 4], F32)
        square = sb("square", [P, 4, VD], F32)
        square_sum = sb("square_sum", [P, 4], F32)
        diff = sb("diff", [P, 4, VD], F32)
        ident_f = sb("ident_f", [P, P], F32)
        ident = sb("ident", [P, P], BF16)
        tri_f = sb("tri_f", [P, P], F32)
        mask_q = [sb(f"mask_q{i}", [P, 512], BF16) for i in range(2)]
        lam_in = sb("lam_in", [P, 4, D], F32)
        lam_prod = sb("lam_prod", [P, 2, D], F32)
        lam_sum = sb("lam_sum", [P, 2, H], F32)
        lam_exp = sb("lam_exp", [P, 2, H], F32)
        neg_lam = sb("neg_lam", [P, H], F32)
        neg_max = [sb(f"neg_max{b}", [P, 2, 2, 2, NPAIR], F32) for b in range(2)]
        neg_hi = [sb(f"neg_hi{b}", [P, 2, 2, 2, NPAIR], F32R) for b in range(2)]
        neg_cols = [sb(f"neg_cols{b}", [P, 2, 4, 2, NPAIR], F32) for b in range(2)]
        neg_rows = [sb(f"neg_rows{b}", [P, P], F32) for b in range(2)]
        rden = sb("rden", [P, 8], F32)
        scaled = sb("scaled", [P, 8, VD], F32)
        score = [psum(f"score{i}", [P, 2, 512]) for i in range(2)]
        mx = [psum(f"mx{i}", [P, 512]) for i in range(2)]
        y = [psum(f"y{i}", [P, 512]) for i in range(2)]

        zeroed, consts_set = sem("zeroed"), sem("consts_set")
        lam_loaded, lam_steps, lam_exped, lam_done = sem("lam_loaded"), sem("lam_steps"), sem("lam_exped"), sem("lam_done")
        loaded = [sem(f"loaded{b}") for b in range(2)]
        max_ready, max_read = sem("max_ready"), sem("max_read")
        split, cols_done, turned, rows_done = sem("split"), sem("cols_done"), sem("turned"), sem("rows_done")
        neg_out, neg_in = [sem(f"neg_out{b}") for b in range(2)], [sem(f"neg_in{b}") for b in range(2)]
        centred, masked, mask_due = sem("centred"), sem("masked"), sem("mask_due")
        scored, exp_done, y_ready, y_step, y_read = sem("scored"), sem("exp_done"), sem("y_ready"), sem("y_step"), sem("y_read")
        NMAXJ = 24
        NG = 4
        block = ctx.enter_context(nc.Block())

        def max_jobs():
            jobs = [(0, m, 4 * p, 4, j) for m in range(2) for p in range(2) for j in range(2)]
            return jobs + [(1, m, 2 * p, 2, j) for m in range(2) for p in range(4) for j in range(2)]

        def batch_pairs(eng, body):
            with eng.Fori(0, B // 2) as i:
                body(i)

        def load_stack(eng, b, par, tensors):
            for i in tensors:
                for j in range(2):
                    for r, part in enumerate((0, 0, 1) if i < 2 else (0, 1, 0)):
                        eng.dma_start(stack[par][i][64 * j + 16 * r:64 * j + 16 * r + DH, :, :].bitcast(F32),
                                      parts[i, part, :, b, :].rearrange("(n j d) t -> j d n t", j=2, d=DH)[j])\
                            .then_inc(loaded[par], 16)

        def load_values(eng, b, par):
            eng.dma_start(val[par][:], values[b].rearrange("t p h v -> p t h v")).then_inc(loaded[par], 16)

        @block.gpsimd
        def _(pool):
            for b in range(2):
                for i in (2, 3):
                    pool.memset(stack[b][i][:].bitcast(F32), 1.0).then_inc(consts_set, 1)
            pool.memset(ident_f[:], 0.0).then_inc(zeroed, 1)
            pool.memset(tri_f[:], 0.0).then_inc(zeroed, 1)
            pool.wait_ge(zeroed, 2)
            pool.affine_select(out=ident_f[:], in_=ident_f[:], compare_op=ALU.not_equal, fill=1.0, base=0,
                               pattern=[[-1, P]], channel_multiplier=1).then_inc(zeroed, 1)
            pool.affine_select(out=tri_f[:], in_=tri_f[:], compare_op=ALU.is_ge, fill=MASKED, base=0,
                               pattern=[[-1, P]], channel_multiplier=1).then_inc(zeroed, 1)
            pool.wait_ge(consts_set, 4)
            for i in range(B // 2):
                if i > 0:
                    pool.wait_ge(y_ready, 16 * i)
                load_stack(pool, 2 * i + 1, 1, range(4))
                load_values(pool, 2 * i + 1, 1)
                with pool.Fori(0, 4) as r:
                    for n in range(6):
                        pool.wait_ge(exp_done, 24 * i + 6 * r + n + 3)
                        pool.sem_inc(mask_due, 1)
                        if n % 3 < 2:
                            v = prob[n][:].rearrange("p j (l h q) -> p (j l) h q", l=2, h=2)[:, :, 0, :]
                        else:
                            v = prob[n][:].rearrange("p j (l q) -> p (j l) q", q=P)
                        pool.affine_select(out=v, in_=v, compare_op=ALU.is_ge, fill=0.0, base=0,
                                           pattern=[[0, v.shape[1]], [1, P]], channel_multiplier=-1).then_inc(masked, 1)

        @block.sync
        def _(sp):
            load_stack(sp, 0, 0, (0, 1))
            load_values(sp, 0, 0)
            for i in range(4):
                sp.dma_start(lam_in[:, i, :], lambdas[i].rearrange("(o h) d -> o (h d)", o=1).broadcast_to([P, D]))\
                    .then_inc(lam_loaded, 16)

            def spread(par, count):
                sp.wait_ge(rows_done, count)
                for qh in range(2):
                    sp.dma_start(neg_dram[par, :, qh * P:(qh + 1) * P], neg_rows[par][64 * qh:64 * qh + 64, :])\
                        .then_inc(neg_out[par], 16)

            def gather(par, count):
                sp.wait_ge(neg_out[par], count)
                for m in range(2):
                    for j in range(2):
                        sp.dma_start(stack[par][m][64 * j + 48:64 * j + 50, :, :].bitcast(F32),
                                     neg_dram[par, 16 * (2 * m + j):16 * (2 * m + j) + 16, :]
                                     .rearrange("(r n) q -> r n q", r=2)).then_inc(neg_in[par], 16)


            def body(i, more):
                for par in range(2):
                    spread(par, 2 * i + par + 1)
                    gather(par, 32 * (i + 1))
                if more:
                    sp.wait_ge(y_ready, 8 * 2 * i + 8)
                    load_stack(sp, 2 * i + 2, 0, range(4))
                    load_values(sp, 2 * i + 2, 0)

            for i in range(B // 2):
                body(i, i < B // 2 - 1)

        @block.tensor
        def _(pe):
            pe.wait_ge(consts_set, 8)

            def max_pass(i, par):
                pe.wait_ge(loaded[par], 16 * 25 * (i + 1))
                for n, (qh, m, p0, np_, j) in enumerate(max_jobs()):
                    pe.wait_ge(max_read, NMAXJ * (2 * i + par) + n + 1)
                    pe.matmul(mx[j][:], ident[:], mask_q[qh][:], start=True, stop=False)
                    nk = P * (qh + 1)
                    for p in range(np_):
                        mm = pe.matmul(mx[j][:, p * nk:(p + 1) * nk],
                                       stack[par][m][64 * j:64 * j + MAX_ROWS, p0 + p, qh * P:(qh + 1) * P],
                                       stack[par][2 + m][64 * j:64 * j + MAX_ROWS, p0 + p, 0:nk],
                                       start=False, stop=(p == np_ - 1))
                    mm.then_inc(max_ready, 1)

            def turn(i, par):
                pe.wait_ge(cols_done, 2 * (2 * i + par) + 2)
                if par == 0:
                    pe.wait_ge(y_read, 16 * i + 2)
                else:
                    pe.wait_ge(rows_done, 2 * i + 1)
                pe.transpose(y[0][:, 0:P], neg_cols[par][:].rearrange("p a m r n -> p (a m r n)"), ident_f[:])\
                    .then_inc(turned, 1)

            def exp_scores(i, par, n):
                g, k = n // 3, n % 3
                pe.wait_ge(exp_done, 12 * (2 * i + par) + n + 1)
                s = score[n % 2]
                for pl in range(2):
                    for m in ((k,) if k < 2 else (0, 1)):
                        for j in range(2):
                            out = s[:, j, pl * NQ:(pl + 1) * NQ] if k < 2 else s[:, j, (2 * m + pl) * P:(2 * m + pl + 1) * P]
                            q0, k0 = (0, 0) if k < 2 else (P, P)
                            mm = pe.matmul(out, stack[par][2 + m][64 * j:64 * j + EXP_ROWS, 2 * g + pl, k0:k0 + P],
                                           stack[par][m][64 * j:64 * j + EXP_ROWS, 2 * g + pl, q0:NQ],
                                           start=True, stop=True)
                mm.then_inc(scored, 1)

            def outputs(i, par, g):
                pe.wait_ge(masked, 12 * (2 * i + par) + 3 * g + 3)
                a = [prob[(3 * g + k) % 6] for k in range(3)]
                for qh in range(2):
                    pe.wait_ge(y_read, 8 * (2 * i + par) + 2 * g + qh + 1)
                    for m in range(2):
                        for hl in range(4):
                            j, pl, h = hl % 2, hl // 2, 4 * g + hl
                            out = y[qh][:, (4 * m + hl) * VW:(4 * m + hl + 1) * VW]
                            mm = pe.matmul(out, a[m][:, j, pl * NQ + qh * P:pl * NQ + (qh + 1) * P],
                                           val[par][:, 0, h, :], start=True, stop=(qh == 0))
                            if qh == 1:
                                mm = pe.matmul(out, a[2][:, j, (2 * m + pl) * P:(2 * m + pl + 1) * P],
                                               val[par][:, 1, h, :], start=False, stop=True)
                    mm.then_inc(y_ready, 1)

            def body(i):
                for par in range(2):
                    max_pass(i, par)
                    turn(i, par)
                for par in range(2):
                    pe.wait_ge(neg_in[par], 64 * (i + 1))
                    for n in range(3 * NG + 3):
                        if n < 3 * NG:
                            exp_scores(i, par, n)
                        if n >= 3 and n % 3 == 2:
                            outputs(i, par, n // 3 - 1)

            batch_pairs(pe, body)

        @block.scalar
        def _(act):
            act.sem_inc(exp_done, 2)
            act.wait_ge(consts_set, 4)
            load_stack(act, 0, 0, (2, 3))
            act.wait_ge(lam_steps, 4)
            act.activation(lam_exp[:], lam_sum[:], ACT.Exp).then_inc(lam_exped, 1)

            def body(i):
                for par in range(2):
                    act.wait_ge(turned, 2 * i + par + 1)
                    act.activation(neg_rows[par][:], y[0][:, 0:P], ACT.Copy).then_inc(rows_done, 1)
                for par in range(2):
                    for n in range(3 * NG):
                        act.wait_ge(scored, 12 * (2 * i + par) + n + 1)
                        act.activation(prob[n % 6][:], score[n % 2][:], ACT.Exp).then_inc(exp_done, 1)

            batch_pairs(act, body)

        @block.vector
        def _(dve):
            dve.sem_inc(max_read, 2)
            dve.sem_inc(y_read, 2)
            dve.wait_ge(zeroed, 4)
            dve.tensor_copy(ident[:], ident_f[:]).then_inc(consts_set, 1)
            for i in range(2):
                dve.memset(mask_q[i][:], 0.0).then_inc(lam_done, 1)
            dve.wait_ge(lam_done, 2)
            for blocks, dst in ((range(4), mask_q[0]), ((1, 3), mask_q[1])):
                for k in blocks:
                    cp = dve.tensor_copy(dst[:, k * P:(k + 1) * P], tri_f[:])
                cp.then_inc(consts_set, 1)
            dve.sem_inc(consts_set, 1)
            dve.wait_ge(lam_loaded, 64)
            for i in range(2):
                dve.tensor_mul(lam_prod[:, i, :], lam_in[:, 2 * i, :], lam_in[:, 2 * i + 1, :]).then_inc(lam_steps, 1)
            dve.wait_ge(lam_steps, 2)
            for i in range(2):
                dve.tensor_reduce(lam_sum[:, i, :], lam_prod[:, i, :].rearrange("p (h d) -> p h d", h=H), AX.X, ALU.add)\
                    .then_inc(lam_steps, 1)
            dve.wait_ge(lam_exped, 1)
            dve.scalar_tensor_tensor(neg_lam[:], lam_exp[:, 1, :], LAMBDA_INIT, lam_exp[:, 0, :],
                                     ALU.subtract, ALU.subtract).then_inc(lam_done, 1)
            dve.wait_ge(lam_done, 3)

            def max_pass(i, par):
                nb = 2 * i + par
                for n, (qh, m, p0, np_, j) in enumerate(max_jobs()):
                    dve.wait_ge(max_ready, NMAXJ * nb + n + 1)
                    dve.tensor_reduce(neg_max[par][:, qh, m, j, p0:p0 + np_],
                                      mx[j][:].rearrange("p (n k) -> p n k", n=np_), AX.X, ALU.max, negate=True)\
                        .then_inc(max_read, 1)
                dve.wait_ge(max_read, NMAXJ * nb + NMAXJ + 2)
                dve.tensor_copy(neg_hi[par][:], neg_max[par][:]).then_inc(split, 1)
                dve.wait_ge(split, nb + 1)
                hi = neg_hi[par][:].bitcast(F32).rearrange("p a m j n -> p a (m j) n")
                full = neg_max[par][:].rearrange("p a m j n -> p a (m j) n")
                dve.tensor_copy(neg_cols[par][:, :, :, 0, :], hi).then_inc(cols_done, 1)
                dve.tensor_sub(neg_cols[par][:, :, :, 1, :], full, hi).then_inc(cols_done, 1)

            def outputs(i, par, g, qh):
                nb = 8 * (2 * i + par) + 2 * g + qh
                yt = y_all[:, 2 * (2 * i + par) + qh, 4 * g:4 * g + 4, :]
                dve.wait_ge(y_ready, nb + 1)
                yv = y[qh][:, 0:8 * VW].rearrange("p (n v) -> p n v", n=8)
                dve.reciprocal(rden[:], yv[:, :, VD]).then_inc(y_step, 1)
                dve.wait_ge(y_step, 3 * nb + 1)
                dve.tensor_mul(rden[:, 4:8], rden[:, 4:8], neg_lam[:, 4 * g:4 * g + 4]).then_inc(y_step, 1)
                dve.wait_ge(y_step, 3 * nb + 2)
                dve.tensor_mul(scaled[:], yv[:, :, 0:VD], rden[:].unsqueeze(2).broadcast_to([P, 8, VD]))\
                    .then_inc(y_read, 1)
                dve.wait_ge(y_read, nb + 3)
                dve.tensor_add(diff[:], scaled[:, 0:4, :], scaled[:, 4:8, :]).then_inc(y_step, 1)
                dve.wait_ge(y_step, 3 * nb + 3)
                dve.tensor_reduce(head_sum[:], diff[:], AX.X, ALU.add).then_inc(centred, 1)
                dve.wait_ge(centred, 6 * nb + 1)
                dve.tensor_scalar(neg_mean[:], head_sum[:], -1.0 / VD, None, ALU.mult).then_inc(centred, 1)
                dve.wait_ge(centred, 6 * nb + 2)
                dve.tensor_add(yt, diff[:], neg_mean[:].unsqueeze(2).broadcast_to([P, 4, VD])).then_inc(centred, 1)
                dve.wait_ge(centred, 6 * nb + 3)
                dve.tensor_mul(square[:], yt, yt).then_inc(centred, 1)
                dve.wait_ge(centred, 6 * nb + 4)
                dve.tensor_reduce(square_sum[:], square[:], AX.X, ALU.add).then_inc(centred, 1)
                dve.wait_ge(centred, 6 * nb + 5)
                dve.tensor_scalar(var_eps[:, 2 * (2 * i + par) + qh, 4 * g:4 * g + 4], square_sum[:], 1.0 / VD, LN_EPS,
                                  ALU.mult, ALU.add).then_inc(centred, 1)
                dve.wait_ge(centred, 6 * nb + 6)

            def body(i):
                for par in range(2):
                    max_pass(i, par)
                for par in range(2):
                    for g in range(NG):
                        for qh in range(2):
                            outputs(i, par, g, qh)

            batch_pairs(dve, body)


def output_stage(nc, x1, c_w, y_all, var_eps, x2, xn2):
    NT = NTOK // P
    YC = 2 * D // P
    with ExitStack() as ctx:
        def sb(name, shape, dt):
            return ctx.enter_context(nc.sbuf_tensor("o_" + name, shape, dt))

        def sem(name):
            return ctx.enter_context(nc.semaphore("o_" + name))

        x_in = sb("x_in", [P, NT, D], F32)
        x_out = sb("x_out", [P, NT, D], F32)
        xn = sb("xn", [P, NT, D], F32)
        w = sb("w", [P, YC, D], F32)
        ident = sb("ident", [P, P], F32)
        scale = sb("scale", [P, NT, H], F32)
        std = sb("std", [P, NT, H], F32)
        rstd = sb("rstd", [P, NT, H], F32)
        yn = sb("yn", [P, NT, 2 * D], F32)
        ynT = sb("ynT", [P, 2, YC, P], F32)
        stats = sb("stats", [P, NT, 6], F32)
        mv = sb("mv", [P, NT, 2], F32)
        var_x = sb("var_x", [P, NT], F32)
        std_x = sb("std_x", [P, NT], F32)
        rstd_x = sb("rstd_x", [P, NT], F32)
        pt = [ctx.enter_context(nc.psum_tensor(f"o_pt{i}", [P, 512], F32)) for i in range(2)]
        po = [ctx.enter_context(nc.psum_tensor(f"o_po{i}", [P, 512], F32)) for i in range(2)]
        loaded, ident_set = sem("loaded"), sem("ident_set")
        chain, std_done, normed, turned, turned_read = sem("chain"), sem("std_done"), sem("normed"), sem("turned"), sem("turned_read")
        projected, x_done, stat_done, stdx_done, xn_done, stored = (sem("projected"), sem("x_done"), sem("stat_done"),
                                                                    sem("stdx_done"), sem("xn_done"), sem("stored"))
        block = ctx.enter_context(nc.Block())

        def y3(t):
            return y_all[:, t, :, :]

        def each(ap):
            return ap.unsqueeze(2).broadcast_to([P, H, VD])

        @block.sync
        def _(sp):
            sp.dma_start(w[:], c_w.rearrange("(c p) n -> p c n", p=P)).then_inc(loaded, 16)
            sp.dma_start(x_in[:], x1.rearrange("b (t p) d -> p (b t) d", p=P)).then_inc(loaded, 16)
            for t in range(NT):
                sp.wait_ge(x_done, t + 1)
                sp.dma_start(x2[t * P:(t + 1) * P, :], x_out[:, t, :]).then_inc(stored, 16)
            for t in range(NT):
                sp.wait_ge(xn_done, t + 1)
                sp.dma_start(xn2[t * P:(t + 1) * P, :], xn[:, t, :]).then_inc(stored, 16)
            sp.wait_ge(stored, 32 * NT)

        @block.gpsimd
        def _(pool):
            pool.memset(ident[:], 0.0).then_inc(ident_set, 1)
            pool.wait_ge(ident_set, 1)
            pool.affine_select(out=ident[:], in_=ident[:], compare_op=ALU.not_equal, fill=1.0, base=0,
                               pattern=[[-1, P]], channel_multiplier=1).then_inc(ident_set, 1)

        @block.vector
        def _(dve):
            c = [0]

            def link(ins):
                c[0] += 1
                ins.then_inc(chain, 1)
                dve.wait_ge(chain, c[0])

            dve.wait_ge(std_done, 1)
            link(dve.reciprocal(rstd[:], std[:]))
            link(dve.tensor_scalar(scale[:], rstd[:], 1.0 - LAMBDA_INIT, None, ALU.mult))
            for t in range(NT):
                dve.tensor_mul(yn[:, t, :].rearrange("p (h v) -> p h v", h=H), y3(t), each(scale[:, t, :]))\
                    .then_inc(normed, 1)
            dve.wait_ge(loaded, 32)
            for t in range(NT):
                dve.wait_ge(projected, t + 1)
                dve.tensor_add(x_out[:, t, :], po[t % 2][:, 0:D], x_in[:, t, :]).then_inc(x_done, 1)
                dve.wait_ge(x_done, t + 1)
                dve.bn_stats(stats[:, t, :], x_out[:, t, :]).then_inc(stat_done, 1)
                dve.wait_ge(stat_done, 2 * t + 1)
                dve.bn_aggr(mv[:, t, :], stats[:, t, :]).then_inc(stat_done, 1)
            dve.wait_ge(stat_done, 2 * NT)
            dve.tensor_scalar(var_x[:], mv[:, :, 1], LN_EPS, None, ALU.add).then_inc(stat_done, 1)
            dve.wait_ge(stdx_done, 1)
            link(dve.reciprocal(rstd_x[:], std_x[:]))
            for t in range(NT):
                dve.tensor_scalar(xn[:, t, :], x_out[:, t, :], mv[:, t, 0:1], rstd_x[:, t:t + 1],
                                  ALU.subtract, ALU.mult).then_inc(xn_done, 1)

        @block.scalar
        def _(act):
            act.activation(std[:], var_eps[:], ACT.Sqrt).then_inc(std_done, 1)
            for t in range(NT):
                act.wait_ge(turned, t + 1)
                if t >= 2:
                    act.wait_ge(projected, t - 1)
                act.activation(ynT[:, t % 2, :, :].rearrange("p c n -> p (c n)"), pt[t % 2][:], ACT.Copy)\
                    .then_inc(turned_read, 1)
            act.wait_ge(stat_done, 2 * NT + 1)
            act.activation(std_x[:], var_x[:], ACT.Sqrt).then_inc(stdx_done, 1)

        @block.tensor
        def _(pe):
            pe.wait_ge(ident_set, 2)
            def turn(t):
                pe.wait_ge(normed, t + 1)
                if t >= 2:
                    pe.wait_ge(turned_read, t - 1)
                for c in range(YC):
                    mm = pe.transpose(pt[t % 2][:, c * P:(c + 1) * P], yn[:, t, c * P:(c + 1) * P], ident[:])
                mm.then_inc(turned, 1)

            turn(0)
            pe.wait_ge(loaded, 32)
            for t in range(NT):
                if t + 1 < NT:
                    turn(t + 1)
                pe.wait_ge(turned_read, t + 1)
                if t >= 2:
                    pe.wait_ge(x_done, t - 1)
                for c in range(YC):
                    mm = pe.matmul(po[t % 2][:, 0:D], ynT[:, t % 2, c, :], w[:, c, :], start=(c == 0), stop=(c == YC - 1))
                mm.then_inc(projected, 1)


E = 8
CAP = 512
FF = 1024
NW = 2048
ST = CAP // P
FC = FF // P
PIECES = 8


def moe_stage(nc, x2, xn2, combine_weights, top_idx, W1, b1, W2, b2, out):
    NT = NTOK // P
    with ExitStack() as ctx:
        def sb(name, shape, dt):
            return ctx.enter_context(nc.sbuf_tensor("e_" + name, shape, dt))

        def sem(name):
            return ctx.enter_context(nc.semaphore("e_" + name))

        def psum(name, shape):
            return ctx.enter_context(nc.psum_tensor("e_" + name, shape, F32))

        idx = sb("idx", [P, ST, E], I32)
        idx_clamped = sb("idx_clamped", [P, ST, E], I32)
        idx_f = sb("idx_f", [P, E, ST], F32)
        iota_i = sb("iota_i", [P, NTOK], I32)
        iota = sb("iota", [P, NTOK], F32)
        weight_rows = sb("weight_rows", [P, E, ST, E], F32)
        weight = [sb(f"weight{i}", [P, ST], F32) for i in range(2)]
        ident = sb("ident", [P, P], F32)
        zeros = sb("zeros", [1, 512], BF16)
        b1_rows = sb("b1_rows", [P, P], F32)
        b1_cols = sb("b1_cols", [P, P], F32)
        b2_all = sb("b2_all", [P, E, D], F32)
        w1 = [sb(f"w1_{i}", [P, DC, FF], F32) for i in range(2)]
        w2 = [sb(f"w2_{i}", [P, FC, D], F32) for i in range(2)]
        g = [sb(f"g{i}", [P, ST, D], F32) for i in range(2)]
        w_hi = [sb(f"w_hi{i}", [P, PIECES, 512], F32R) for i in range(2)]
        w_lo = [sb(f"w_lo{i}", [P, PIECES, 512], F32R) for i in range(2)]
        gT_hi = sb("gT_hi", [P, DC, CAP], F32R)
        gT_lo = sb("gT_lo", [P, DC, CAP], F32R)
        h = sb("h", [P, 2, CAP], F32)
        h_hi = sb("h_hi", [P, FC, CAP], F32R)
        h_lo = sb("h_lo", [P, FC, CAP], F32R)
        biased = sb("biased", [P, 2, D], F32)
        v_hi = sb("v_hi", [P, 2, D], F32R)
        v_lo = sb("v_lo", [P, 2, D], F32R)
        onehot = sb("onehot", [P, 2, NTOK], F32R)
        x_in = sb("x_in", [P, NT, D], F32)
        x_out = sb("x_out", [P, NT, D], F32)
        ph = [psum(f"ph{i}", [P, CAP]) for i in range(2)]
        shared = [psum(f"shared{i}", [P, CAP]) for i in range(2)]
        pt = shared[1]
        po = [shared[i][:, 0:D] for i in (0, 1, 0, 0)]
        acc = psum("acc", [P, NT, D])

        idx_loaded, b_loaded, b2_loaded, x_loaded = sem("idx_loaded"), sem("b_loaded"), sem("b2_loaded"), sem("x_loaded")
        w_loaded = [sem(f"w_loaded{i}") for i in range(2)]
        gathered = [sem(f"gathered{i}") for i in range(2)]
        weights_in = [sem(f"weights_in{i}") for i in range(2)]
        ident_set, iota_set, consts_set, idx_set = sem("ident_set"), sem("iota_set"), sem("consts_set"), sem("idx_set")
        b1_turned, b1_done = sem("b1_turned"), sem("b1_done")
        turned, gT_hi_done, gT_done = sem("turned"), sem("gT_hi_done"), sem("gT_done")
        w_hi_done, w_split, h_hi_done, h_split = sem("w_hi_done"), sem("w_split"), sem("h_hi_done"), sem("h_split")
        hidden, gelu_done = sem("hidden"), sem("gelu_done")
        experted, bias_done, hi_done, v_done = sem("experted"), sem("bias_done"), sem("hi_done"), sem("v_done")
        weight_set, onehot_set, scattered = sem("weight_set"), sem("onehot_set"), sem("scattered")
        summed, stored = sem("summed"), sem("stored")
        block = ctx.enter_context(nc.Block())

        def raw_piece(par, k):
            w = w1[par] if k < PIECES // 2 else w2[par]
            return w[:].rearrange("p a b -> p (a b)")[:, 512 * (k % 4):512 * (k % 4) + 512]

        def w1_part(part, c, f):
            return part[:, 2 * c + f // 4, P * (f % 4):P * (f % 4) + P]

        def w2_part(part, f):
            return part[:, 4 + f // 2, D * (f % 2):D * (f % 2) + D]

        def expert_pairs(eng, body):
            with eng.Fori(0, E // 2 - 1) as i:
                body(i, True)
            body(E // 2 - 1, False)

        @block.sync
        def _(sp):
            sp.dma_start(idx[:], top_idx.rearrange("(p t) e -> p t e", t=ST)).then_inc(idx_loaded, 16)
            sp.wait_ge(consts_set, 1)
            sp.dma_start(b1_rows[0:E * FC, :], b1.rearrange("e (f p) -> (e f) p", p=P)).then_inc(b_loaded, 16)

            def load(n, par):
                sp.dma_start(w1[par][:], W1[n].rearrange("(c p) f -> p c f", p=P)).then_inc(w_loaded[par], 16)
                sp.dma_start(w2[par][:], W2[n].rearrange("(f p) d -> p f d", p=P)).then_inc(w_loaded[par], 16)

            load(0, 0)
            sp.wait_ge(gT_done, DC)
            sp.dma_start(b2_all[:], b2.rearrange("(o e) d -> o e d", o=1).broadcast_to([P, E, D])).then_inc(b2_loaded, 16)
            load(1, 1)
            sp.dma_start(x_in[:], x2.rearrange("(t p) d -> p t d", p=P)).then_inc(x_loaded, 16)
            with sp.Fori(0, E // 2 - 1) as i:
                for par in range(2):
                    sp.wait_ge(w_split, PIECES * (2 * i + par + 1))
                    load(2 * i + par + 2, par)
            for t in range(NT):
                sp.wait_ge(summed, t + 1)
                sp.dma_start(out[t * P:(t + 1) * P, :], x_out[:, t, :]).then_inc(stored, 16)
            sp.wait_ge(stored, 16 * NT)

        @block.gpsimd
        def _(pool):
            pool.memset(ident[:], 0.0).then_inc(ident_set, 1)
            pool.iota(iota_i[:], pattern=[[1, NTOK]], base=0, channel_multiplier=0).then_inc(iota_set, 1)
            pool.wait_ge(ident_set, 1)
            pool.affine_select(out=ident[:], in_=ident[:], compare_op=ALU.not_equal, fill=1.0, base=0,
                               pattern=[[-1, P]], channel_multiplier=1).then_inc(ident_set, 1)
            pool.wait_ge(idx_set, 1)
            for n in range(E):
                par = n % 2
                if n >= 2:
                    pool.wait_ge(turned, DC * (n - 1))
                    pool.wait_ge(weight_set, n - 1)
                for t in range(ST):
                    pool.indirect_dma_start(g[par][:, t, :], None, xn2,
                                            bass.IndirectOffsetOnAxis(ap=idx_clamped[:, t, n:n + 1], axis=0))\
                        .then_inc(gathered[par], 16)
                for t in range(ST):
                    pool.indirect_dma_start(weight_rows[:, n, t, :], None, combine_weights,
                                            bass.IndirectOffsetOnAxis(ap=idx[:, t, n:n + 1], axis=0))\
                        .then_inc(weights_in[par], 16)

        @block.tensor
        def _(pe):
            pe.wait_ge(consts_set, 2)
            for k in range(NT // 2):
                pe.matmul(acc[:, 2 * k:2 * k + 2, :], zeros[0:1, 0:P], zeros[0:1, :], start=True, stop=False)
            pe.wait_ge(ident_set, 2)
            pe.wait_ge(b_loaded, 16)
            pe.transpose(shared[0][:, 0:P], b1_rows[:], ident[:]).then_inc(b1_turned, 1)
            pe.wait_ge(b1_done, 1)

            def turn(n, i, par, c):
                if c == 0:
                    pe.wait_ge(gathered[par], 16 * ST * (i + 1))
                else:
                    pe.wait_ge(gT_done, DC * n + c)
                for t in range(ST):
                    mm = pe.transpose(pt[:, t * P:(t + 1) * P], g[par][:, t, c * P:(c + 1) * P], ident[:])
                mm.then_inc(turned, 1)

            def scatter(n, t):
                pe.wait_ge(v_done, ST * n + t + 1)
                pe.wait_ge(onehot_set, ST * n + t + 1)
                for k in range(NT):
                    for v in (v_hi, v_lo):
                        mm = pe.matmul(acc[:, k, :], onehot[:, t % 2, k * P:(k + 1) * P], v[:, t % 2, :],
                                       start=False, stop=False)
                mm.then_inc(scattered, 1)

            def body(i, more):
                for par in range(2):
                    n = 2 * i + par
                    pe.wait_ge(w_split, PIECES * (n + 1))
                    pe.wait_ge(gT_done, DC * n + DC)
                    for f in range(FC):
                        pe.wait_ge(gelu_done, FC * n + f + 1)
                        for c in range(DC):
                            for k, (w, g_part) in enumerate(((w_hi, gT_hi), (w_hi, gT_lo), (w_lo, gT_hi))):
                                mm = pe.matmul(ph[f % 2][:], w1_part(w[par], c, f), g_part[:, c, :],
                                               start=(c + k == 0), stop=(c == DC - 1 and k == 2))
                        mm.then_inc(hidden, 1)
                    pe.wait_ge(h_split, FC * n + FC + 2)
                    for t in range(ST):
                        pe.wait_ge(bias_done, ST * n + (0, 0, 1, 3)[t] + 1)
                        for f in range(FC):
                            for k, (h_part, w) in enumerate(((h_hi, w_hi), (h_hi, w_lo), (h_lo, w_hi))):
                                mm = pe.matmul(po[t], h_part[:, f, t * P:(t + 1) * P], w2_part(w[par], f),
                                               start=(f + k == 0), stop=(f == FC - 1 and k == 2))
                        mm.then_inc(experted, 1)
                        if t == 3 and (more or par == 0):
                            turn(n + 1, i + par, 1 - par, 1)
                        if t >= 1:
                            scatter(n, t - 1)
                        if t == 2 and (more or par == 0):
                            pe.wait_ge(bias_done, ST * n + 1 + 2)
                            turn(n + 1, i + par, 1 - par, 0)
                    scatter(n, ST - 1)

            turn(0, 0, 0, 0)
            turn(0, 0, 0, 1)
            expert_pairs(pe, body)
            for k in range(NT // 2):
                mm = pe.matmul(acc[:, 2 * k:2 * k + 2, :], zeros[0:1, 0:P], zeros[0:1, :], start=False, stop=True)
            mm.then_inc(scattered, 1)

        @block.scalar
        def _(act):
            act.sem_inc(gelu_done, 2)
            act.wait_ge(b1_turned, 1)
            act.activation(b1_cols[:], shared[0][:, 0:P], ACT.Copy).then_inc(b1_done, 1)
            act.wait_ge(b1_done, 1)

            def rows(n, c):
                act.wait_ge(turned, DC * n + c + 1)
                act.activation(gT_hi[:, c, :], pt[:], ACT.Copy).then_inc(gT_hi_done, 1)

            def weights(n, i, par, pieces):
                act.wait_ge(w_loaded[par], 32 * (i + 1))
                for k in pieces:
                    act.activation(w_hi[par][:, k, :], raw_piece(par, k), ACT.Copy).then_inc(w_hi_done, 1)

            def body(i, more):
                for par in range(2):
                    n = 2 * i + par
                    for f in range(FC):
                        act.wait_ge(hidden, FC * n + f + 1)
                        act.wait_ge(h_split, FC * n + f + 1)
                        act.activation(h[:, f % 2, :], ph[f % 2][:], ACT.Gelu_apprx_tanh,
                                       bias=b1_cols[:, bass.ds(FC * n + f, 1)]).then_inc(gelu_done, 1)
                    if more or par == 0:
                        weights(n + 1, i + par, 1 - par, range(0, 6))
                        rows(n + 1, 0)
                        weights(n + 1, i + par, 1 - par, range(6, PIECES))
                        rows(n + 1, 1)

            weights(0, 0, 0, range(PIECES))
            rows(0, 0)
            rows(0, 1)
            expert_pairs(act, body)

        @block.vector
        def _(dve):
            dve.sem_inc(bias_done, 1)
            dve.sem_inc(scattered, 2)
            dve.sem_inc(h_split, 2)
            dve.memset(b1_rows[:], 0.0).then_inc(consts_set, 1)
            dve.memset(zeros[:], 0.0).then_inc(consts_set, 1)
            dve.wait_ge(idx_loaded, 16)
            dve.tensor_scalar(idx_clamped[:], idx[:], NTOK - 1, None, ALU.min).then_inc(idx_set, 1)
            dve.tensor_copy(idx_f[:], idx[:].rearrange("p t e -> p e t")).then_inc(idx_set, 1)
            dve.wait_ge(iota_set, 1)
            dve.tensor_copy(iota[:], iota_i[:]).then_inc(iota_set, 1)
            dve.wait_ge(iota_set, 2)
            dve.wait_ge(idx_set, 2)

            def rows(n, c):
                dve.wait_ge(gT_hi_done, DC * n + c + 1)
                dve.tensor_sub(gT_lo[:, c, :], pt[:], gT_hi[:, c, :].bitcast(F32)).then_inc(gT_done, 1)

            def weights(n, par, pieces):
                for k in pieces:
                    dve.wait_ge(w_hi_done, PIECES * n + k + 1)
                    dve.tensor_sub(w_lo[par][:, k, :], raw_piece(par, k), w_hi[par][:, k, :].bitcast(F32)).then_inc(w_split, 1)

            def body(i, more):
                for par in range(2):
                    n = 2 * i + par
                    for f in range(FC):
                        dve.wait_ge(gelu_done, FC * n + f + 3)
                        dve.tensor_copy(h_hi[:, f, :], h[:, f % 2, :]).then_inc(h_hi_done, 1)
                        dve.wait_ge(h_hi_done, FC * n + f + 1)
                        dve.tensor_sub(h_lo[:, f, :], h[:, f % 2, :], h_hi[:, f, :].bitcast(F32)).then_inc(h_split, 1)
                    dve.wait_ge(weights_in[par], 16 * ST * (i + 1))
                    dve.tensor_copy(weight[par][:], weight_rows[:, bass.ds(n, 1), :, bass.ds(n, 1)]).then_inc(weight_set, 1)
                    dve.wait_ge(weight_set, n + 1)
                    for t in range(ST):
                        dve.wait_ge(scattered, ST * n + t + 1)
                        dve.tensor_scalar(onehot[:, t % 2, :], iota[:], idx_f[:, bass.ds(n, 1), t], None, ALU.is_equal)\
                            .then_inc(onehot_set, 1)
                        dve.wait_ge(experted, ST * n + t + 1)
                        dve.tensor_add(biased[:, t % 2, :], po[t], b2_all[:, bass.ds(n, 1), :])\
                            .then_inc(bias_done, 1)
                        dve.wait_ge(bias_done, ST * n + t + 2)
                        dve.tensor_scalar(v_hi[:, t % 2, :], biased[:, t % 2, :], weight[par][:, t:t + 1], None, ALU.mult)\
                            .then_inc(hi_done, 1)
                        dve.wait_ge(hi_done, ST * n + t + 1)
                        dve.scalar_tensor_tensor(v_lo[:, t % 2, :], biased[:, t % 2, :], weight[par][:, t:t + 1],
                                                 v_hi[:, t % 2, :].bitcast(F32), ALU.mult, ALU.subtract).then_inc(v_done, 1)
                        if more or par == 0:
                            weights(n + 1, 1 - par, range(2 * t, 2 * t + 2))
                            if t >= 2:
                                rows(n + 1, t - 2)

            weights(0, 0, range(PIECES))
            rows(0, 0)
            rows(0, 1)
            dve.wait_ge(b2_loaded, 16)
            expert_pairs(dve, body)
            dve.wait_ge(scattered, ST * E + 3)
            dve.wait_ge(x_loaded, 16)
            for t in range(NT):
                dve.tensor_add(x_out[:, t, :], acc[:, t, :], x_in[:, t, :]).then_inc(summed, 1)


_INS = ["x", "ctx_1024", "mask_Bx1x1xS2_ik0", "L0_xattn_Wq", "L0_xattn_bq", "L0_xattn_Wk", "L0_xattn_bk",
        "L0_xattn_Wv", "L0_xattn_bv", "L0_xattn_Wo", "L0_xattn_bo",
        "L0_attn_q1_w", "L0_attn_q2_w", "L0_attn_k1_w", "L0_attn_k2_w", "L0_attn_v_w", "L0_attn_c_w",
        "L0_attn_lambda_q1", "L0_attn_lambda_k1", "L0_attn_lambda_q2", "L0_attn_lambda_k2",
        "L0_ffn_combine_weights", "L0_ffn_top_idx", "L0_ffn_W1", "L0_ffn_b1", "L0_ffn_W2", "L0_ffn_b2"]


def kernel(**inputs):
    import numpy as _np
    import concourse.bacc as _bacc
    from concourse import mybir as _mybir
    from concourse.bass_utils import run_bass_kernel_spmd as _run

    nc = _bacc.Bacc("TRN2", target_bir_lowering=False, num_devices=1)
    arrays, t = {}, {}
    for name in _INS:
        a = _np.ascontiguousarray(inputs[name])
        arrays[f"in_{name}"] = a
        t[name] = nc.dram_tensor(f"in_{name}", a.shape, _mybir.dt.from_np(a.dtype), kind="ExternalInput").ap()
    out = nc.dram_tensor("out_0", (B, NQ, D), F32, kind="ExternalOutput").ap()
    build(nc, t, out)
    r = _run(nc, [arrays], core_ids=[0])
    return r.results[0]["out_0"]


def cross_attention(nc, t, x1):
    q_stacks = nc.dram_tensor("q_stacks", (B, QU, P, 2, NQ), F32, kind="Internal").ap()
    mask_rows = nc.dram_tensor("mask_rows", (2, B, NK), F32, kind="Internal").ap()
    query_stage(nc, t["x"], t["L0_xattn_Wq"], t["L0_xattn_bq"], t["mask_Bx1x1xS2_ik0"], q_stacks, mask_rows)
    cross_stage(nc, t["x"], t["ctx_1024"], t["L0_xattn_Wk"], t["L0_xattn_bk"], t["L0_xattn_Wv"], t["L0_xattn_bv"],
                t["L0_xattn_Wo"], t["L0_xattn_bo"], q_stacks, mask_rows, x1)


def self_attention(nc, t, x1, x2, xn2):
    parts = nc.dram_tensor("attn_parts", (4, 2, D, NTOK), F32, kind="Internal").ap()
    values = nc.dram_tensor("attn_values", (NTOK // P, P, H, VW), F32, kind="Internal").ap()
    neg_dram = nc.dram_tensor("attn_neg", (2, 64, NQ), F32, kind="Internal").ap()
    names = ("L0_attn_q1_w", "L0_attn_q2_w", "L0_attn_k1_w", "L0_attn_k2_w")
    project_stage(nc, x1, [t[n] for n in names], t["L0_attn_v_w"], parts, values)
    lambdas = [t["L0_attn_lambda_" + n] for n in ("q1", "k1", "q2", "k2")]
    with nc.sbuf_tensor("y_all", [P, NTOK // P, H, VD], F32) as y_all, \
            nc.sbuf_tensor("head_var_eps", [P, NTOK // P, H], F32) as var_eps:
        diff_stage(nc, parts.rearrange("i r n (b t) -> i r n b t", b=B), values.rearrange("(b t) p h v -> b t p h v", b=B),
                   lambdas, neg_dram, y_all, var_eps)
        output_stage(nc, x1, t["L0_attn_c_w"], y_all, var_eps, x2, xn2)


def build(nc, t, out):
    x1 = nc.dram_tensor("x1", (B, NQ, D), F32, kind="Internal").ap()
    x2 = nc.dram_tensor("x2", (NTOK, D), F32, kind="Internal").ap()
    xn2 = nc.dram_tensor("xn2", (NTOK, D), F32, kind="Internal").ap()
    cross_attention(nc, t, x1)
    self_attention(nc, t, x1, x2, xn2)
    moe_stage(nc, x2, xn2, t["L0_ffn_combine_weights"], t["L0_ffn_top_idx"], t["L0_ffn_W1"], t["L0_ffn_b1"],
              t["L0_ffn_W2"], t["L0_ffn_b2"], out.rearrange("b q d -> (b q) d"))
```
